# Optimizing a Trainium2 kernel written in Bass

```python
import numpy as np
import jax
import jax.numpy as jnp

def _softmax(x, axis=-1):
    return jax.nn.softmax(x, axis=axis)

def _gelu(x):
    return jax.nn.gelu(x, approximate=True)

def _silu(x):
    return jax.nn.silu(x)

def _sigmoid(x):
    return jax.nn.sigmoid(x)

def _layernorm(x, axis=-1, eps=1e-05):
    m = jnp.mean(x, axis=axis, keepdims=True)
    v = jnp.var(x, axis=axis, keepdims=True)
    return (x - m) / jnp.sqrt(v + eps)

def _scatter_add(tgt, idx, src, axis=0):
    return tgt.at[idx].add(src)

def _segment_sum(src, seg, n):
    return jax.ops.segment_sum(src, seg, n)
kernel_name = 'mk_xattn_ffn_d1_seqx_r8_1b8aec'

def setup_inputs(seed: int=0):
    np.random.seed(seed)
    _w = jnp.asarray

    def _rec_inputs():
        import jax
        import jax.numpy as jnp
        _rk = jax.random.key(seed)
        x = -0.0002928 + 1 * jax.random.normal(jax.random.fold_in(_rk, 1), (8, 128, 512), jnp.float32)
        _lenS = 128 - jax.random.randint(jax.random.fold_in(_rk, 7), (8,), 0, max(1, 128 // 4) + 1, jnp.int32)
        _lenS2 = 128 - jax.random.randint(jax.random.fold_in(_rk, 8), (8,), 0, max(1, 128 // 4) + 1, jnp.int32)
        _ctx_4096P = jax.random.normal(jax.random.fold_in(_rk, 11), (8, 16, 512), jnp.float32)
        _ctx_4096c = jax.random.dirichlet(jax.random.fold_in(_rk, 511), 0.3 * jnp.ones((16,), jnp.float32), (8, 128))
        _ctx_4096t = jnp.einsum('bsk,bkd->bsd', _ctx_4096c, _ctx_4096P)
        _ctx_4096t = _ctx_4096t * jax.lax.rsqrt(jnp.mean(jnp.square(_ctx_4096t)) + 1e-12) * 0.953939
        ctx_4096 = -2.8382e-05 + 0.999851 * (_ctx_4096t + 0.3 * jax.random.normal(jax.random.fold_in(_rk, 611), (8, 128, 512), jnp.float32))
        _validS = jnp.arange(128)[None, :] < _lenS[:, None]
        _validS2 = jnp.arange(128)[None, :] < _lenS2[:, None]
        _causal = jnp.tril(jnp.ones((128, 128), dtype=bool))
        mask_1x1xSxS2_ff0 = jnp.where(jnp.ones((1, 1, 128, 128), dtype=bool), 0.0, -1000000000.0).astype(jnp.float32)
        return (x, ctx_4096, mask_1x1xSxS2_ff0)
    x, ctx_4096, mask_1x1xSxS2_ff0 = _rec_inputs()

    def _L0_xattn_setup():
        import jax, jax.numpy as jnp
        import numpy as np
        NUM_HEADS = 32
        NUM_KV_HEADS = 8
        HEAD_DIM = 128
        HIDDEN = 512
        EPS = 1e-05

        def rmsnorm(x, w, eps=EPS):
            xf = x.astype(jnp.float32)
            var = jnp.mean(xf * xf, axis=-1, keepdims=True)
            return w * (xf * jax.lax.rsqrt(var + eps)).astype(x.dtype)
        key = jax.random.key(seed)
        ks = jax.random.split(key, 10)
        B, Q, KV = (1, 128, 6404)
        s = 1.0 / np.sqrt(HIDDEN)
        return {'hidden_states': jax.random.normal(ks[0], (B, Q, HIDDEN), jnp.float32), 'cross_attention_states': jax.random.normal(ks[1], (B, KV, HIDDEN), jnp.float32), 'attention_mask': jnp.zeros((B, 1, Q, KV), jnp.float32), 'q_proj_w': jax.random.normal(ks[2], (NUM_HEADS * HEAD_DIM, HIDDEN), jnp.float32) * s, 'k_proj_w': jax.random.normal(ks[3], (NUM_KV_HEADS * HEAD_DIM, HIDDEN), jnp.float32) * s, 'v_proj_w': jax.random.normal(ks[4], (NUM_KV_HEADS * HEAD_DIM, HIDDEN), jnp.float32) * s, 'o_proj_w': jax.random.normal(ks[5], (HIDDEN, NUM_HEADS * HEAD_DIM), jnp.float32) * s, 'q_norm_w': jnp.ones((HEAD_DIM,), jnp.float32), 'k_norm_w': jnp.ones((HEAD_DIM,), jnp.float32)}
    _L0_xattn_all = _L0_xattn_setup()
    _L0_xattn_in = {k: v for k, v in _L0_xattn_all.items() if k in ('q_proj_w', 'k_proj_w', 'v_proj_w', 'o_proj_w', 'q_norm_w', 'k_norm_w')}
    del _L0_xattn_all

    def _L0_ffn_setup():
        import jax, jax.numpy as jnp
        import numpy as np
        NF4_CODE = jnp.array([-1.0, -0.6961928009986877, -0.5250730514526367, -0.39491748809814453, -0.28444138169288635, -0.18477343022823334, -0.09105003625154495, 0.0, 0.07958029955625534, 0.16093020141124725, 0.24611230194568634, 0.33791524171829224, 0.44070982933044434, 0.5626170039176941, 0.7229568362236023, 1.0], dtype=jnp.float32)
        BLOCKSIZE = 64

        def nf4_quant_dequant(w):
            shape = w.shape
            flat = w.reshape(-1, BLOCKSIZE)
            absmax = jnp.max(jnp.abs(flat), axis=1, keepdims=True)
            normalized = flat / jnp.where(absmax == 0, 1.0, absmax)
            bounds = (NF4_CODE[:-1] + NF4_CODE[1:]) * 0.5
            idx = jnp.searchsorted(bounds, normalized)
            return (NF4_CODE[idx] * absmax).reshape(shape)
        key = jax.random.key(seed)
        k1, k2, k3, kx = jax.random.split(key, 4)
        D, H = (512, 1376)
        scale = 0.02
        w1 = jax.random.normal(k1, (H, D), jnp.float32) * scale
        w2 = jax.random.normal(k2, (H, D), jnp.float32) * scale
        w3 = jax.random.normal(k3, (D, H), jnp.float32) * scale
        x = jax.random.normal(kx, (2, 256, D), jnp.float32)
        return {'x': x, 'w1': w1, 'w2': w2, 'w3': w3}
    _L0_ffn_all = _L0_ffn_setup()
    _L0_ffn_in = {k: v for k, v in _L0_ffn_all.items() if k in ('w1', 'w2', 'w3')}
    del _L0_ffn_all
    return {'x': x, 'ctx_4096': ctx_4096, 'mask_1x1xSxS2_ff0': mask_1x1xSxS2_ff0, 'L0_xattn_q_proj_w': _L0_xattn_in['q_proj_w'], 'L0_xattn_k_proj_w': _L0_xattn_in['k_proj_w'], 'L0_xattn_v_proj_w': _L0_xattn_in['v_proj_w'], 'L0_xattn_o_proj_w': _L0_xattn_in['o_proj_w'], 'L0_xattn_q_norm_w': _L0_xattn_in['q_norm_w'], 'L0_xattn_k_norm_w': _L0_xattn_in['k_norm_w'], 'L0_ffn_w1': _L0_ffn_in['w1'], 'L0_ffn_w2': _L0_ffn_in['w2'], 'L0_ffn_w3': _L0_ffn_in['w3']}

def reference(x, ctx_4096, mask_1x1xSxS2_ff0, L0_xattn_q_proj_w, L0_xattn_k_proj_w, L0_xattn_v_proj_w, L0_xattn_o_proj_w, L0_xattn_q_norm_w, L0_xattn_k_norm_w, L0_ffn_w1, L0_ffn_w2, L0_ffn_w3):
    import jax
    import jax.numpy as jnp

    def _L0_xattn_ref(hidden_states, cross_attention_states, attention_mask, q_proj_w, k_proj_w, v_proj_w, o_proj_w, q_norm_w, k_norm_w):
        import jax, jax.numpy as jnp
        import numpy as np
        NUM_HEADS = 32
        NUM_KV_HEADS = 8
        HEAD_DIM = 128
        HIDDEN = 512
        EPS = 1e-05

        def rmsnorm(x, w, eps=EPS):
            xf = x.astype(jnp.float32)
            var = jnp.mean(xf * xf, axis=-1, keepdims=True)
            return w * (xf * jax.lax.rsqrt(var + eps)).astype(x.dtype)
        B, Q, _ = hidden_states.shape
        KV = cross_attention_states.shape[1]
        n_rep = NUM_HEADS // NUM_KV_HEADS
        q = (hidden_states @ q_proj_w.T).reshape(B, Q, NUM_HEADS, HEAD_DIM).transpose(0, 2, 1, 3)
        k = (cross_attention_states @ k_proj_w.T).reshape(B, KV, NUM_KV_HEADS, HEAD_DIM).transpose(0, 2, 1, 3)
        v = (cross_attention_states @ v_proj_w.T).reshape(B, KV, NUM_KV_HEADS, HEAD_DIM).transpose(0, 2, 1, 3)
        q = rmsnorm(q, q_norm_w)
        k = jnp.repeat(k, n_rep, axis=1)
        v = jnp.repeat(v, n_rep, axis=1)
        k = rmsnorm(k, k_norm_w)
        scale = 1.0 / np.sqrt(HEAD_DIM)
        scores = jnp.einsum('bhqd,bhkd->bhqk', q, k) * scale + attention_mask
        attn = jax.nn.softmax(scores.astype(jnp.float32), axis=-1).astype(q.dtype)
        out = jnp.einsum('bhqk,bhkd->bhqd', attn, v)
        out = out.transpose(0, 2, 1, 3).reshape(B, Q, NUM_HEADS * HEAD_DIM)
        return out @ o_proj_w.T

    def _L0_ffn_ref(x, w1, w2, w3):
        import jax, jax.numpy as jnp
        import numpy as np
        NF4_CODE = jnp.array([-1.0, -0.6961928009986877, -0.5250730514526367, -0.39491748809814453, -0.28444138169288635, -0.18477343022823334, -0.09105003625154495, 0.0, 0.07958029955625534, 0.16093020141124725, 0.24611230194568634, 0.33791524171829224, 0.44070982933044434, 0.5626170039176941, 0.7229568362236023, 1.0], dtype=jnp.float32)
        BLOCKSIZE = 64

        def nf4_quant_dequant(w):
            shape = w.shape
            flat = w.reshape(-1, BLOCKSIZE)
            absmax = jnp.max(jnp.abs(flat), axis=1, keepdims=True)
            normalized = flat / jnp.where(absmax == 0, 1.0, absmax)
            bounds = (NF4_CODE[:-1] + NF4_CODE[1:]) * 0.5
            idx = jnp.searchsorted(bounds, normalized)
            return (NF4_CODE[idx] * absmax).reshape(shape)
        dq1 = nf4_quant_dequant(w1)
        dq2 = nf4_quant_dequant(w2)
        dq3 = nf4_quant_dequant(w3)
        gate = jnp.einsum('bsd,hd->bsh', x, dq1)
        up = jnp.einsum('bsd,hd->bsh', x, dq2)
        h = jax.nn.silu(gate) * up
        return jnp.einsum('bsh,dh->bsd', h, dq3)
    x = x + _L0_xattn_ref(_layernorm(x, axis=-1), ctx_4096, mask_1x1xSxS2_ff0, L0_xattn_q_proj_w, L0_xattn_k_proj_w, L0_xattn_v_proj_w, L0_xattn_o_proj_w, L0_xattn_q_norm_w, L0_xattn_k_norm_w)
    x = x + _L0_ffn_ref(_layernorm(x, axis=-1), L0_ffn_w1, L0_ffn_w2, L0_ffn_w3)
    return x

_drawn_inputs = setup_inputs


def setup_inputs(seed=0):
    import zlib

    import numpy as np

    out = dict(_drawn_inputs(seed))
    spreads = {'L0_xattn_q_norm_w': (1.0, 0.2), 'L0_xattn_k_norm_w': (1.0, 0.2)}
    factors = {}
    for name, (base, spread) in spreads.items():
        noise = np.random.default_rng([zlib.crc32(name.encode()), seed]).standard_normal(out[name].shape)
        drawn = base * np.exp(spread * noise) if base else spread * noise
        out[name] = jnp.asarray(drawn.astype(out[name].dtype))
    for name, factor in factors.items():
        out[name] = (out[name] * factor).astype(out[name].dtype)
    return out
```

```python
import concourse.bass as bass
from concourse import mybir
from contextlib import ExitStack
import numpy as np

F32 = mybir.dt.float32
F32R = mybir.dt.float32r
BF16 = mybir.dt.bfloat16
ALU = mybir.AluOpType
ACT = mybir.ActivationFunctionType
AX = mybir.AxisListType

P = 128
B = 8
S = 128
D = 512
KT = D // P
HD = 128
G = 8
J = 4
N = G * B
F = 1376
FT = F // P
FR = F - FT * P
TILES = FT + 1
EPS = 1e-5
LN_EPS = 1e-5
GC = D // HD
KV_SLABS = G // GC
KV_UNITS = 2 * KV_SLABS * B

CODE = np.array([-1.0, -0.6961928009986877, -0.5250730514526367, -0.39491748809814453,
                 -0.28444138169288635, -0.18477343022823334, -0.09105003625154495, 0.0,
                 0.07958029955625534, 0.16093020141124725, 0.24611230194568634, 0.33791524171829224,
                 0.44070982933044434, 0.5626170039176941, 0.7229568362236023, 1.0], np.float32)
BOUND = ((CODE[:-1] + CODE[1:]) * np.float32(0.5)).astype(np.float32)
ZERO = 7
BOUNDS = len(BOUND)
BLK = 64
FLAT = F * D // P
QC = 512
QREST = FLAT - G * QC
EARLY = [512, 448, 448]
assert sum(EARLY) == QREST and all(n % BLK == 0 for n in EARLY)
Q0 = 3 * len(EARLY)
ORDER = [7, 0, 8, 1, 9, 2, 10, 3, 11, 4, 12, 5, 13, 6, 14]
RING = 5


def build(nc, x, ctxT, mask, wqT, wkT, wvT, woT, qnw, knw, w1, w2, w3, out):
    weights = [w1, w2, w3]
    dq_dram = [nc.dram_tensor(f"dq{j + 1}_scratch", [P, FLAT], F32).ap() for j in range(3)]
    v_dram = nc.dram_tensor("v_scratch", [G, P, B, HD], F32).ap()
    dq1 = dq_dram[0].rearrange("p n -> (p n)").rearrange("(h d) -> h d", d=D)
    dq2 = dq_dram[1].rearrange("p n -> (p n)").rearrange("(h d) -> h d", d=D)
    dq3 = dq_dram[2].rearrange("p n -> (p n)").rearrange("(r p h) -> p r h", r=KT, p=P)
    wq_v = wqT.rearrange("(k p) n -> p k n", p=P)
    wk_v = wkT.rearrange("(k p) n -> p k n", p=P)
    wv_v = wvT.rearrange("(k p) n -> p k n", p=P)
    wo_v = woT.rearrange("(h p) n -> p h n", p=P)
    ctx_v = ctxT.rearrange("(k p) n -> p k n", p=P)

    es = ExitStack()
    with es:
        def sb(name, shape, dt=F32):
            return es.enter_context(nc.sbuf_tensor(name, shape, dt))

        def ps(name):
            return es.enter_context(nc.psum_tensor(name, [P, 512], F32))

        def sem(name):
            return es.enter_context(nc.semaphore(name))

        resid = sb("resid", [P, B, D])
        xT_hi = sb("xT_hi", [P, KT, B * S], F32R)
        xT_lo = sb("xT_lo", [P, KT, B * S], F32R)
        early = sb("early", [P, 2 * KT * B * S], F32R)
        ctx_hi = early[:, 0:KT * B * S].rearrange("p (k n) -> p k n", k=KT)
        ctx_lo = early[:, KT * B * S:].rearrange("p (k n) -> p k n", k=KT)
        wo_hi = early[:, 0:2048].rearrange("p (j n) -> p j n", j=J)
        wo_lo = early[:, 2048:4096].rearrange("p (j n) -> p j n", j=J)
        o_hi_sb = early[:, 4096:5120].rearrange("p (r n) -> p r n", r=2)
        o_lo_sb = early[:, 5120:6144].rearrange("p (r n) -> p r n", r=2)
        hT_hi = early[:, 0:2048].rearrange("p (r n) -> p r n", r=2)
        hT_lo = early[:, 2048:4096].rearrange("p (r n) -> p r n", r=2)
        kT = sb("kT", [P, G, B * S])
        ring = sb("ring", [P, 2, 2, KT, 512], F32R)
        wT = ring[:, :, :, :, :].rearrange("p s l k n -> p s (l k n)")
        raw = sb("raw", [P, KT, 512])
        wo_raw = sb("wo_raw", [P, J, 512])
        v_sb = sb("v_sb", [P, B, HD])
        wqk = sb("wqk", [P, 1])
        qn_sb = sb("qn_sb", [P, 1])
        kn_sb = sb("kn_sb", [P, 1])
        mask_sb = sb("mask_sb", [P, S])
        ident = sb("ident", [P, P])
        neg_half = sb("neg_half", [P, B])
        hd_eps = sb("hd_eps", [P, J])
        q_sb = sb("q_sb", [P, 2, 512])
        sq_sb = sb("sq_sb", [P, 512])
        qT_sb = sb("qT_sb", [P, 2, 512])
        sp_sb = sb("sp_sb", [P, 4, 512])
        s_sb = sp_sb[:, 0:2, :]
        p_sb = sp_sb[:, 2:4, :]
        pT_sb = sb("pT_sb", [P, 2, 512])
        ctx_raw = [wo_raw[:, :, :], sp_sb[:, :, :]]
        ssq = sb("ssq", [P, 4, J])
        var = sb("var", [P, J])
        ln_var_sb = sb("ln_var_sb", [P, B])
        rq = sb("rq", [P, 4, J])
        nmax = sb("nmax", [P, 2, J])
        psum_ = sb("psum_", [P, 2, J])
        rsum = sb("rsum", [P, 2, J])
        stats = sb("stats", [P, B, 6])
        mv = sb("mv", [P, B, 2])
        rstd = sb("rstd", [P, B])
        nf_raw = sb("nf_raw", [P, QC])
        nf_n = sb("nf_n", [P, QC])
        nf_sign = sb("nf_sign", [P, RING, QC], BF16)
        nf_pos = sb("nf_pos", [P, QC])
        nf_neg = sb("nf_neg", [P, QC])
        nf_dq = sb("nf_dq", [P, QC])
        amax = sb("amax", [P, QC // BLK])
        safe = sb("safe", [P, 3, QC // BLK])
        rmax = sb("rmax", [P, QC // BLK])
        wn = kT[:, :, :].rearrange("p g n -> p (g n)")[:, 0:2 * 1536].rearrange("p (s c n) -> p s c n", s=2, c=3)
        silu_sb = s_sb
        h_sb = p_sb

        proj_ps = [ps("proj_ps0"), ps("proj_ps1")]
        turn_ps = ps("turn_ps")
        s_ps = [ps("s_ps0"), ps("s_ps1")]
        pT_ps = ps("pT_ps")
        oT_ps = ps("oT_ps")
        attn_ps = ps("attn_ps")

        x_in, small_in, mask_in = sem("x_in"), sem("small_in"), sem("mask_in")
        ctx_in = [sem(f"ctx_in{k}") for k in range(KT + 1)]
        raw_in = [sem(f"raw_in{k}") for k in range(KT)]
        wo_in = [sem(f"wo_in{j}") for j in range(J)]
        v_in = [sem("v_in0"), sem("v_in1")]
        v_out = [sem("v_out0"), sem("v_out1")]
        nf_in, nf_out = sem("nf_in"), sem("nf_out")
        wn_in = [sem("wn_in0"), sem("wn_in1")]
        y_out = sem("y_out")
        const_zero, const_set, const_done, wqk_done = (sem(n) for n in ("const_zero", "const_set", "const_done", "wqk_done"))
        ctx_hi_done, ctx_lo_done = sem("ctx_hi_done"), sem("ctx_lo_done")
        slab_hi, slab_lo = sem("slab_hi"), sem("slab_lo")
        wo_hi_done, wo_lo_done = sem("wo_hi_done"), sem("wo_lo_done")
        kv_ready, kv_squared, kv_ssq, kv_var, kv_rk = (sem(n) for n in ("kv_ready", "kv_squared", "kv_ssq", "kv_var", "kv_rk"))
        k_normed, k_turned, k_stored, v_copied = (sem(n) for n in ("k_normed", "k_turned", "k_stored", "v_copied"))
        ln_stats, ln_mv, ln_var, ln_rstd, ln_x, ln_turned, ln_hi, ln_lo = (
            sem(n) for n in ("ln_stats", "ln_mv", "ln_var", "ln_rstd", "ln_x", "ln_turned", "ln_hi", "ln_lo"))
        q_ready, q_copied, q_squared, q_ssq, q_var, q_rq = (
            sem(n) for n in ("q_ready", "q_copied", "q_squared", "q_ssq", "q_var", "q_rq"))
        qT_ready, qT_copied, s_ready, s_scaled, s_max, p_exp, p_rsum, p_normed = (
            sem(n) for n in ("qT_ready", "qT_copied", "s_ready", "s_scaled", "s_max", "p_exp", "p_rsum", "p_normed"))
        pT_ready, pT_copied, oT_ready, oT_hi, oT_lo, attn_ready, attn_added = (
            sem(n) for n in ("pT_ready", "pT_copied", "oT_ready", "oT_hi", "oT_lo", "attn_ready", "attn_added"))
        nf_amax, nf_safe, nf_rmax, nf_normed, nf_signed, nf_chained, nf_summed, nf_scaled = (
            sem(n) for n in ("nf_amax", "nf_safe", "nf_rmax", "nf_normed", "nf_signed", "nf_chained", "nf_summed", "nf_scaled"))
        w_turned, w_hi, w_lo, gate_ready, up_ready, silu_done, h_done, h_hi, h_lo, down_ready, down_added = (
            sem(n) for n in ("w_turned", "w_hi", "w_lo", "gate_ready", "up_ready", "silu_done", "h_done",
                             "h_hi", "h_lo", "down_ready", "down_added"))
        block = es.enter_context(nc.Block())

        def wait(eng, s, count):
            if not isinstance(count, int) or count > 0:
                eng.wait_ge(s, count)

        def live(n):
            return not isinstance(n, int) or 0 <= n < N

        def slab_slot(m):
            return ring[:, m % 2, :, :, :]

        def heads(ap):
            return ap.rearrange("p (j n) -> p j n", j=J)

        def kv_kind(c):
            return c // B, c % B, c < KV_SLABS * B

        kv_ps = [proj_ps[0], proj_ps[1], s_ps[0], s_ps[1]]
        wT_ps = [turn_ps, pT_ps]
        down_ps = [oT_ps, attn_ps]

        def n_par(s, lag):
            return (s - lag) % 2

        def has_tile(t):
            return not isinstance(t, int) or 0 <= t < TILES

        def rows_of(t):
            return FR if isinstance(t, int) and t == TILES - 1 else P

        def wT_part(par, c, l, M):
            at = 2048 * l + 512 * c
            return wT[:, par, at:at + KT * M].rearrange("p (k m) -> p k m", k=KT)

        def w3_part(par, l, M):
            at = 2048 * l + 1024
            return wT[0:M, par, at:at + D]

        def WN_COUNT(t):
            return 48 * (t // 2 + 1)

        def chunk_ap(tensors, g, j):
            return tensors[j][:, bass.ds(g * QC, QC)] if not isinstance(g, int) else tensors[j][:, g * QC:(g + 1) * QC]

        def early_ap(tensors, q):
            j, e = divmod(q, len(EARLY))
            at = G * QC + sum(EARLY[:e])
            return tensors[j][:, at:at + EARLY[e]]

        def cols_of(q):
            return EARLY[q % len(EARLY)] if q < Q0 else QC

        SIGNS = [(0, 0, 5), (0, 5, 10), (0, 10, 15), (1, 0, 5), (1, 5, 10), (1, 10, 15), (2, 0, 8), (2, 8, 15)]

        def spread(lo, hi, parts):
            cut = [lo + (hi - lo) * i // parts for i in range(parts + 1)]
            return list(zip(cut[:-1], cut[1:]))

        @block.sync
        def _(sp):
            def load_slab(m, src):
                for k in range(KT):
                    wait(sp, slab_lo, (m - 1) * KT + k + 1)
                    sp.dma_start(raw[:, k, :], src[:, k, :]).then_inc(raw_in[k], 16)

            def load_wo(g):
                for j in range(J):
                    wait(sp, wo_lo_done, (g - 1) * J + j + 1)
                    sp.dma_start(wo_raw[:, j, :], wo_v[:, g * J + j, :]).then_inc(wo_in[j], 16)

            def load_v(g, half):
                wait(sp, oT_ready, g * B - (4 if half == 0 else 0))
                sp.dma_start(v_sb[:, 4 * half:4 * half + 4, :], v_dram[g, :, 4 * half:4 * half + 4, :])\
                    .then_inc(v_in[half], 16)

            def nf_load(q, src, cols):
                wait(sp, nf_normed, q)
                sp.dma_start(nf_raw[:, 0:cols], src).then_inc(nf_in, 16)

            def nf_store(q, dst, cols):
                wait(sp, nf_scaled, q + 1)
                sp.dma_start(dst, nf_dq[:, 0:cols]).then_inc(nf_out, 16)

            kv_src = [wk_v[:, :, 0:512], wk_v[:, :, 512:1024], wv_v[:, :, 0:512], wv_v[:, :, 512:1024]]
            for k in range(KT):
                sp.dma_start(ctx_raw[0][:, k, :], ctx_v[:, k, 0:512]).then_inc(ctx_in[k], 16)
                sp.dma_start(raw[:, k, :], kv_src[0][:, k, :]).then_inc(raw_in[k], 16)
            def nf_early(q):
                nf_load(q, early_ap(weights, q) if q < Q0 else chunk_ap(weights, 0, 0), cols_of(q))
                if q >= 2:
                    nf_store(q - 2, early_ap(dq_dram, q - 2), cols_of(q - 2))

            nf_early(0)
            sp.dma_start(ctx_raw[1], ctx_v[:, :, 512:1024]).then_inc(ctx_in[KT], 16)
            load_slab(1, kv_src[1])
            sp.dma_start(resid[:, :, :], x.rearrange("b s d -> s b d")).then_inc(x_in, 16)
            sp.dma_start(qn_sb[:, :], qnw.rearrange("(p a) -> p a", a=1)).then_inc(small_in, 16)
            sp.dma_start(kn_sb[:, :], knw.rearrange("(p a) -> p a", a=1)).then_inc(small_in, 16)
            sp.dma_start(mask_sb[:, :], mask[0, 0, :, :]).then_inc(mask_in, 16)
            nf_early(1)
            load_slab(2, kv_src[2])
            for q in range(2, Q0 + 1):
                nf_early(q)
                if q == 3:
                    load_slab(3, kv_src[3])
                if q == 5:
                    load_slab(4, wq_v[:, :, 0:512])
            sp.wait_ge(ctx_lo_done, 2 * KT)
            for p in range(2):
                sp.wait_ge(v_out[p], 16 * KV_SLABS * B // 2)

            def body(g, last):
                q = Q0 + 3 * g
                load_v(g, 0)
                load_wo(g)
                if not last:
                    load_slab(5 + g, wq_v[:, :, bass.ds((g + 1) * 512, 512)])
                load_v(g, 1)
                if isinstance(g, int) and g == 0:
                    nf_store(q - 1, early_ap(dq_dram, Q0 - 1), cols_of(Q0 - 1))
                else:
                    nf_store(q - 1, chunk_ap(dq_dram, g - 1, 2), QC)
                nf_load(q + 1, chunk_ap(weights, g, 1), QC)
                nf_store(q, chunk_ap(dq_dram, g, 0), QC)
                nf_load(q + 2, chunk_ap(weights, g, 2), QC)
                nf_store(q + 1, chunk_ap(dq_dram, g, 1), QC)
                if not last:
                    nf_load(q + 3, chunk_ap(weights, g + 1, 0), QC)

            body(0, False)
            with sp.Fori(1, G - 1) as g:
                body(g, False)
            body(G - 1, True)
            nf_store(Q0 + 3 * G - 1, chunk_ap(dq_dram, G - 1, 2), QC)

            sp.wait_ge(nf_out, 16 * (Q0 + 3 * G))
            sp.wait_ge(s_ready, N)

            def load_tile(t, par, M):
                wait(sp, w_turned, 3 * (t - 1))
                rows = bass.ds(t * P, M)
                sp.dma_start(wn[0:M, par, 0, :], dq1[rows, :]).then_inc(wn_in[par], 16)
                sp.dma_start(wn[0:M, par, 1, :], dq2[rows, :]).then_inc(wn_in[par], 16)
                sp.dma_start(wn[:, par, 2, 0:KT * M].rearrange("p (r m) -> p r m", r=KT), dq3[:, :, rows])\
                    .then_inc(wn_in[par], 16)

            for t in range(2):
                load_tile(t, t, P)
            with sp.Fori(1, FT // 2) as tt:
                for par in range(2):
                    load_tile(tt * 2 + par, par, P)
            load_tile(TILES - 1, (TILES - 1) % 2, FR)
            for m in range(B):
                sp.wait_ge(down_added, (TILES - 1) * B + m + 1)
                sp.dma_start(out[m, :, :], resid[:, m, :]).then_inc(y_out, 16)
            sp.wait_ge(y_out, 16 * B)

        def at(g, s, lag):
            return g + (s - lag) // B, (s - lag) % B, B * g + s - lag

        @block.tensor
        def _(pe):
            def turn(bank, src, cols, rows=P):
                for k in range(len(src)):
                    mm = pe.transpose(bank[0:cols, k * rows:(k + 1) * rows], src[k], ident[0:rows, 0:rows])
                return mm

            def three_pass(bank, pairs):
                for n, (a_hi, a_lo, b_hi, b_lo) in enumerate(pairs):
                    pe.matmul(bank, a_hi, b_hi, start=(n == 0), stop=False)
                    pe.matmul(bank, a_hi, b_lo, start=False, stop=False)
                    mm = pe.matmul(bank, a_lo, b_hi, start=False, stop=(n == len(pairs) - 1))
                return mm

            def tokens(ap, k, b):
                return ap[:, k, b * S:(b + 1) * S]

            def kv(c):
                m, b, _ = kv_kind(c)
                pe.wait_ge(slab_lo, KT * (m + 1))
                pe.wait_ge(ctx_lo_done, KT * (b // 4 + 1))
                if 4 <= c < KV_SLABS * B + 4:
                    pe.wait_ge(k_normed, c - 3)
                elif c >= 4:
                    pe.wait_ge(v_copied, c - 3 - KV_SLABS * B)
                three_pass(kv_ps[c % 4][:, :], [
                    (tokens(ctx_hi, k, b), tokens(ctx_lo, k, b), slab_slot(m)[:, 0, k, :], slab_slot(m)[:, 1, k, :])
                    for k in range(KT)]).then_inc(kv_ready, 1)

            def turn_k(c):
                pe.wait_ge(k_normed, c + 1)
                wait(pe, k_stored, c)
                turn(turn_ps, [q_sb[:, c % 2, j * HD:(j + 1) * HD] for j in range(J)], P).then_inc(k_turned, 1)

            def turn_x(n):
                pe.wait_ge(ln_x, n + 1)
                if n == 0:
                    pe.wait_ge(k_stored, KV_SLABS * B)
                elif n == B:
                    pe.wait_ge(qT_copied, N)
                wait(pe, ln_lo, n)
                turn(turn_ps, [qT_sb[:, n % 2, k * P:(k + 1) * P] for k in range(KT)], P).then_inc(ln_turned, 1)

            pe.wait_ge(const_done, 1)
            for c in range(KV_UNITS):
                kv(c)
                if 0 <= c - 3 < KV_SLABS * B:
                    turn_k(c - 3)
                if 0 <= c - 20 < B:
                    turn_x(c - 20)

            def step(g, s):
                _, _, n = at(g, s, 3)
                if live(n):
                    pe.wait_ge(p_normed, n + 1)
                    wait(pe, pT_copied, n)
                    turn(pT_ps, [p_sb[:, n_par(s, 3), j * S:(j + 1) * S] for j in range(J)], P).then_inc(pT_ready, 1)

                gg, b, n = at(g, s, 4)
                if live(n):
                    pe.wait_ge(oT_lo, n + 1)
                    wait(pe, attn_added, n)
                    for j in range(J):
                        pe.wait_ge(wo_lo_done, gg * J + j + 1)
                        r = n_par(s, 4)
                        oh, ol = (t[:, r, j * S:(j + 1) * S] for t in (o_hi_sb, o_lo_sb))
                        pe.matmul(attn_ps[:, :], oh, wo_hi[:, j, :], start=(j == 0), stop=False)
                        pe.matmul(attn_ps[:, :], oh, wo_lo[:, j, :], start=False, stop=False)
                        mm = pe.matmul(attn_ps[:, :], ol, wo_hi[:, j, :], start=False, stop=(j == J - 1))
                    mm.then_inc(attn_ready, 1)

                _, _, n = at(g, s, 1)
                if live(n):
                    pe.wait_ge(q_copied, n + 1)
                    wait(pe, qT_copied, n)
                    if isinstance(n, int) and n == 0:
                        pe.wait_ge(ln_lo, B)
                    turn(turn_ps, [q_sb[:, n_par(s, 1), j * HD:(j + 1) * HD] for j in range(J)], P).then_inc(qT_ready, 1)

                gg, b, n = at(g, s, 3)
                if live(n):
                    pe.wait_ge(pT_copied, n + 1)
                    pe.wait_ge(v_in[b // 4], 16 * (gg + 1))
                    wait(pe, oT_lo, n)
                    pe.matmul(oT_ps[:, :], v_sb[:, b, :], pT_sb[:, n_par(s, 3), :], start=True, stop=True)\
                        .then_inc(oT_ready, 1)

                gg, b, n = at(g, s, 1)
                if live(n):
                    pe.wait_ge(qT_copied, n + 1)
                    wait(pe, s_scaled, n - 1)
                    if isinstance(n, int) and n == 0:
                        pe.wait_ge(k_stored, KV_SLABS * B)
                    for j in range(J):
                        mm = pe.matmul(s_ps[n_par(s, 1)][:, j * S:(j + 1) * S],
                                       qT_sb[:, n_par(s, 1), j * S:(j + 1) * S],
                                       kT[:, gg, b * S:(b + 1) * S], start=True, stop=True)
                    mm.then_inc(s_ready, 1)

                gg, b, n = at(g, s, 0)
                if live(n):
                    pe.wait_ge(slab_lo, KT * (2 * KV_SLABS + gg + 1))
                    wait(pe, q_squared, n - 1)
                    if isinstance(n, int) and n < 2:
                        pe.wait_ge(v_copied, KV_SLABS * B)
                    if isinstance(n, int) and n < B:
                        pe.wait_ge(ln_lo, n + 1)
                    slab = ring[:, gg % 2, :, :, :]
                    three_pass(proj_ps[n_par(s, 0)][:, :], [
                        (tokens(xT_hi, k, b), tokens(xT_lo, k, b), slab[:, 0, k, :], slab[:, 1, k, :])
                        for k in range(KT)]).then_inc(q_ready, 1)

            for s in range(B):
                step(0, s)
            with pe.Fori(1, G) as g:
                for s in range(B):
                    step(g, s)
            for s in range(4):
                step(G, s)

            def turn_w(t, par, M, parts):
                pe.wait_ge(wn_in[par], WN_COUNT(t))
                for c in parts:
                    u = 3 * t + c
                    wait(pe, w_lo, u - 1)
                    if isinstance(t, int) and t == 0 and c == 0:
                        pe.wait_ge(ln_lo, 2 * B)
                    bank = wT_ps[(3 * par + c) % 2]
                    if c < 2:
                        mm = turn(bank, [wn[0:M, par, c, k * P:(k + 1) * P] for k in range(KT)], P, M)
                    else:
                        mm = turn(bank, [wn[:, par, 2, r * M:(r + 1) * M] for r in range(KT)], M, P)
                    mm.then_inc(w_turned, 1)

            def gate_up(t, par, M, half):
                v = 2 * t + half
                for c, (bank, free, ready) in enumerate(((proj_ps[half], silu_done, gate_ready),
                                                         (s_ps[half], h_done, up_ready))):
                    pe.wait_ge(w_lo, 3 * t + c + 1)
                    wait(pe, free, v - 1)
                    three_pass(bank[0:M, :], [
                        (wT_part(par, c, 0, M)[:, k, :], wT_part(par, c, 1, M)[:, k, :],
                         xT_hi[:, k, half * 512:(half + 1) * 512], xT_lo[:, k, half * 512:(half + 1) * 512])
                        for k in range(KT)]).then_inc(ready, 1)

            def down(t, par, M, m):
                pe.wait_ge(h_lo, 2 * t + m // 4 + 1)
                pe.wait_ge(w_lo, 3 * t + 3)
                wait(pe, down_added, B * t + m - 1)
                hh, hl = (a[0:M, par, m * S:(m + 1) * S] for a in (hT_hi, hT_lo))
                three_pass(down_ps[m % 2][:, :], [(hh, hl, w3_part(par, 0, M), w3_part(par, 1, M))])\
                    .then_inc(down_ready, 1)

            for n in range(B, 2 * B):
                turn_x(n)

            def ffn(t, par):
                if has_tile(t - 1):
                    turn_w(t - 1, 1 - par, rows_of(t - 1), [2])
                if has_tile(t):
                    turn_w(t, par, rows_of(t), [0, 1])
                for half in range(2):
                    if has_tile(t - 1):
                        gate_up(t - 1, 1 - par, rows_of(t - 1), half)
                    if has_tile(t - 2):
                        for m in range(4 * half, 4 * half + 4):
                            down(t - 2, par, rows_of(t - 2), m)

            for t in range(4):
                ffn(t, t % 2)
            with pe.Fori(2, FT // 2) as tt:
                for par in range(2):
                    ffn(tt * 2 + par, par)
            for t in range(FT, TILES + 2):
                ffn(t, t % 2)

        @block.scalar
        def _(act):
            def signs(q, cols, lo, hi):
                for t in range(lo, hi):
                    i = ORDER[t]
                    n = BOUNDS * q + t
                    edge = BOUND[i] if i >= ZERO else np.nextafter(BOUND[i], np.float32(1))
                    if t == 0 or t == lo:
                        act.wait_ge(nf_normed, q + 1)
                    wait(act, nf_chained, n - RING + 1)
                    act.activation(nf_sign[:, t % RING, 0:cols], nf_n[:, 0:cols], ACT.Sign, bias=-float(edge))\
                        .then_inc(nf_signed, 1)

            def slab_part(m, k, dst, free, count):
                act.wait_ge(raw_in[k], 16 * (m + 1))
                wait(act, free, count)
                act.activation(dst[:, 0, k, :], raw[:, k, :], ACT.Copy).then_inc(slab_hi, 1)

            def turn_x_hi(n, b):
                act.wait_ge(ln_turned, n + 1)
                act.activation(xT_hi[:, :, b * S:(b + 1) * S], heads(turn_ps[:, :]), ACT.Copy).then_inc(ln_hi, 1)

            for k in range(KT):
                act.wait_ge(ctx_in[k], 16)
                act.activation(ctx_hi[:, k, 0:512], ctx_raw[0][:, k, :], ACT.Copy).then_inc(ctx_hi_done, 1)
                slab_part(0, k, slab_slot(0), kv_ready, 0)
            act.wait_ge(ctx_in[KT], 16)
            for k in range(KT):
                act.activation(ctx_hi[:, k, 512:1024], ctx_raw[1][:, k, :], ACT.Copy).then_inc(ctx_hi_done, 1)
            for k in range(KT):
                slab_part(1, k, slab_slot(1), kv_ready, 0)

            def store_k(c):
                m, b, _ = kv_kind(c)
                act.wait_ge(k_turned, c + 1)
                act.wait_ge(wqk_done, 2)
                act.activation(kT[:, m * GC:(m + 1) * GC, b * S:(b + 1) * S], heads(turn_ps[:, :]), ACT.Copy,
                               scale=wqk[:, 0:1]).then_inc(k_stored, 1)

            for c in range(KV_UNITS):
                m, b, is_k = kv_kind(c)
                if m >= 1 and m < 4 and b < KT:
                    slab_part(m + 1, b, slab_slot(m + 1), kv_ready, B * m)
                if is_k:
                    act.wait_ge(kv_ready, c + 1)
                    wait(act, kv_ssq, c)
                    act.activation(sq_sb[:, :], kv_ps[c % 4][:, :], ACT.Square).then_inc(kv_squared, 1)
                else:
                    v = c - KV_SLABS * B
                    act.wait_ge(kv_ready, c + 1)
                    wait(act, v_out[v % 2], 16 * (v // 2))
                    act.activation(pT_sb[:, c % 2, :], kv_ps[c % 4][:, :], ACT.Copy).then_inc(v_copied, 1)
                    act.wait_ge(v_copied, v + 1)
                    h0 = (m - KV_SLABS) * GC
                    act.dma_start(v_dram[h0:h0 + GC, :, b, :].rearrange("g p d -> p g d"), heads(pT_sb[:, c % 2, :]))\
                        .then_inc(v_out[v % 2], 16)
                if 0 <= c - 4 < KV_SLABS * B:
                    store_k(c - 4)
                if 0 <= c - 21 < B:
                    turn_x_hi(c - 21, c - 21)
                lo, hi = spread(0, Q0 * BOUNDS, KV_UNITS)[c]
                for t in range(lo, hi):
                    signs(t // BOUNDS, cols_of(t // BOUNDS), t % BOUNDS, t % BOUNDS + 1)

            def step(g, s):
                parts = spread(SIGNS[s][1], SIGNS[s][2], 3)
                q = Q0 + 3 * g + SIGNS[s][0]
                mine = not isinstance(g, int) or g < G

                _, _, n = at(g, s, 1)
                if live(n):
                    r = n_par(s, 1)
                    act.wait_ge(q_ready, n + 1)
                    wait(act, qT_ready, n - 1)
                    if isinstance(n, int) and n == 0:
                        act.wait_ge(k_turned, KV_SLABS * B)
                    act.activation(q_sb[:, r, :], proj_ps[r][:, :], ACT.Copy).then_inc(q_copied, 1)
                    wait(act, q_ssq, n)
                    act.activation(sq_sb[:, :], proj_ps[r][:, :], ACT.Square).then_inc(q_squared, 1)

                _, _, n = at(g, s, 3)
                if live(n):
                    act.wait_ge(pT_ready, n + 1)
                    wait(act, oT_ready, n - 1)
                    if isinstance(n, int) and n < 2:
                        act.wait_ge(v_out[n], 16 * KV_SLABS * B // 2)
                    act.activation(pT_sb[:, n_par(s, 3), :], pT_ps[:, :], ACT.Copy).then_inc(pT_copied, 1)

                _, _, n = at(g, s, 2)
                if live(n):
                    r = n_par(s, 2)
                    act.wait_ge(s_max, n + 1)
                    wait(act, pT_ready, n - 1)
                    for j in range(J):
                        e = act.activation(p_sb[:, r, j * S:(j + 1) * S], s_sb[:, r, j * S:(j + 1) * S], ACT.Exp,
                                           bias=nmax[:, r, j:j + 1], accum_out=psum_[:, r, j:j + 1])
                    e.then_inc(p_exp, 1)

                if mine:
                    signs(q, QC, *parts[0])

                _, _, n = at(g, s, 1)
                if live(n):
                    act.wait_ge(qT_ready, n + 1)
                    wait(act, s_ready, n - 1)
                    act.activation(qT_sb[:, n_par(s, 1), :], turn_ps[:, :], ACT.Copy).then_inc(qT_copied, 1)

                if mine and s < KT and not (isinstance(g, int) and g == G - 1):
                    first = isinstance(g, int) and g == 0
                    slab_part(2 * KV_SLABS + 1 + g, s, ring[:, (g + 1) % 2, :, :, :],
                              kv_ready if first else q_ready, KV_UNITS if first else B * g)
                if mine:
                    signs(q, QC, *parts[1])

                _, _, n = at(g, s, 3)
                if live(n):
                    act.wait_ge(oT_ready, n + 1)
                    wait(act, attn_ready, n - 1)
                    if isinstance(n, int) and n == 0:
                        act.wait_ge(kv_ready, KV_UNITS)
                    act.activation(o_hi_sb[:, n_par(s, 3), :], oT_ps[:, :], ACT.Copy).then_inc(oT_hi, 1)

                if mine and s == 3:
                    for j in range(J):
                        act.wait_ge(wo_in[j], 16 * (g + 1))
                        wait(act, attn_ready, B * g)
                        act.activation(wo_hi[:, j, :], wo_raw[:, j, :], ACT.Copy).then_inc(wo_hi_done, 1)
                if mine:
                    signs(q, QC, *parts[2])

            for s in range(B):
                step(0, s)
            with act.Fori(1, G - 1) as g:
                for s in range(B):
                    step(g, s)
            for s in range(B):
                step(G - 1, s)
            for s in range(4):
                step(G, s)

            for n in range(B, 2 * B):
                turn_x_hi(n, n - B)

            def split_w(t, par, M, parts):
                for c in parts:
                    u = 3 * t + c
                    act.wait_ge(w_turned, u + 1)
                    if c < 2:
                        wait(act, up_ready, 2 * (t - 1))
                        src = wT_ps[(3 * par + c) % 2][:, 0:KT * M].rearrange("p (k m) -> p k m", k=KT)
                        act.activation(wT_part(par, c, 0, M), src, ACT.Copy).then_inc(w_hi, 1)
                    else:
                        wait(act, down_ready, B * (t - 1))
                        act.activation(w3_part(par, 0, M), wT_ps[(3 * par + c) % 2][0:M, :], ACT.Copy).then_inc(w_hi, 1)

            def silu(t, M, half):
                v = 2 * t + half
                act.wait_ge(gate_ready, v + 1)
                wait(act, h_done, v - 1)
                act.activation(silu_sb[0:M, half, :], proj_ps[half][0:M, :], ACT.Silu).then_inc(silu_done, 1)

            def hidden_hi(t, par, M, half):
                v = 2 * t + half
                act.wait_ge(h_done, v + 1)
                wait(act, down_ready, B * (t - 1))
                act.activation(hT_hi[0:M, par, half * 512:(half + 1) * 512], h_sb[0:M, half, :], ACT.Copy)\
                    .then_inc(h_hi, 1)

            def ffn(t, par):
                if has_tile(t - 1):
                    split_w(t - 1, 1 - par, rows_of(t - 1), [2])
                if has_tile(t):
                    split_w(t, par, rows_of(t), [0, 1])
                if has_tile(t - 1):
                    for half in range(2):
                        silu(t - 1, rows_of(t - 1), half)
                        hidden_hi(t - 1, 1 - par, rows_of(t - 1), half)

            for t in range(4):
                ffn(t, t % 2)
            with act.Fori(2, FT // 2) as tt:
                for par in range(2):
                    ffn(tt * 2 + par, par)
            for t in range(FT, TILES + 1):
                ffn(t, t % 2)

        @block.vector
        def _(dve):
            def nf_prep(q, slot, cols):
                nb = cols // BLK
                dve.wait_ge(nf_in, 16 * (q + 1))
                wait(dve, nf_scaled, q - 2)
                dve.tensor_reduce(amax[:, 0:nb], nf_raw[:, 0:cols].rearrange("p (b e) -> p b e", e=BLK),
                                  AX.X, ALU.max, apply_absolute_value=True).then_inc(nf_amax, 1)
                dve.wait_ge(nf_amax, q + 1)
                dve.scalar_tensor_tensor(safe[:, slot, 0:nb], amax[:, 0:nb], 0.0, amax[:, 0:nb],
                                         op0=ALU.is_equal, op1=ALU.add).then_inc(nf_safe, 1)
                dve.wait_ge(nf_safe, q + 1)
                dve.reciprocal(rmax[:, 0:nb], safe[:, slot, 0:nb]).then_inc(nf_rmax, 1)

            def chain(q, cols, lo, hi):
                for t in range(lo, hi):
                    i = ORDER[t]
                    n = BOUNDS * q + t
                    dve.wait_ge(nf_signed, n + 1)
                    if t < 2:
                        wait(dve, nf_summed, q)
                    else:
                        dve.wait_ge(nf_chained, n - 1)
                    up = i >= ZERO
                    acc = nf_pos if up else nf_neg
                    code = float(CODE[i + 1]) if up else -float(CODE[i])
                    op = ALU.max if up else ALU.min
                    sign = nf_sign[:, t % RING, 0:cols]
                    if t < 2:
                        ins = dve.tensor_scalar(acc[:, 0:cols], sign, code, 0.0, ALU.mult, op)
                    else:
                        ins = dve.scalar_tensor_tensor(acc[:, 0:cols], sign, code, acc[:, 0:cols], op0=ALU.mult, op1=op)
                    ins.then_inc(nf_chained, 1)

            def layer_stats(n, b):
                dve.bn_stats(stats[:, b, :], resid[:, b, :]).then_inc(ln_stats, 1)
                dve.wait_ge(ln_stats, n + 1)
                dve.bn_aggr(mv[:, b, :], stats[:, b, :]).then_inc(ln_mv, 1)

            def layer_norm(n, b):
                dve.wait_ge(ln_rstd, 1 if n < B else 2)
                wait(dve, ln_turned, n - 1)
                if n == B:
                    dve.wait_ge(s_ready, N)
                dve.tensor_scalar(qT_sb[:, n % 2, :], resid[:, b, :], mv[:, b, 0:1], rstd[:, b:b + 1],
                                  ALU.subtract, ALU.mult).then_inc(ln_x, 1)

            def turn_x_lo(n, b):
                dve.wait_ge(ln_hi, n + 1)
                dve.tensor_tensor(xT_lo[:, :, b * S:(b + 1) * S], heads(turn_ps[:, :]),
                                  xT_hi[:, :, b * S:(b + 1) * S], ALU.subtract).then_inc(ln_lo, 1)

            for k in range(KT):
                dve.wait_ge(ctx_hi_done, k + 1)
                dve.tensor_tensor(ctx_lo[:, k, 0:512], ctx_raw[0][:, k, :], ctx_hi[:, k, 0:512], ALU.subtract)\
                    .then_inc(ctx_lo_done, 1)
            for k in range(KT):
                dve.wait_ge(ctx_hi_done, KT + k + 1)
                dve.tensor_tensor(ctx_lo[:, k, 512:1024], ctx_raw[1][:, k, :], ctx_hi[:, k, 512:1024], ALU.subtract)\
                    .then_inc(ctx_lo_done, 1)
            nf_prep(0, 0, cols_of(0))
            dve.wait_ge(small_in, 32)
            dve.tensor_tensor(wqk[:, :], qn_sb[:, :], kn_sb[:, :], ALU.mult).then_inc(wqk_done, 1)
            dve.wait_ge(wqk_done, 1)
            dve.tensor_scalar(wqk[:, :], wqk[:, :], float(np.sqrt(HD)), None, ALU.mult).then_inc(wqk_done, 1)

            def ssq_k(c):
                dve.wait_ge(kv_squared, c + 1)
                wait(dve, kv_rk, c - 3)
                dve.tensor_reduce(ssq[:, c % 4, :], heads(sq_sb[:, :]), AX.X, ALU.add).then_inc(kv_ssq, 1)

            def norm_k(c):
                dve.wait_ge(kv_rk, c + 1)
                wait(dve, k_turned, c - 1)
                dve.tensor_tensor(heads(q_sb[:, c % 2, :]), heads(kv_ps[c % 4][:, :]),
                                  rq[:, c % 4, :].unsqueeze(2).to_broadcast([P, J, HD]), ALU.mult).then_inc(k_normed, 1)

            dve.wait_ge(x_in, 16)
            for c in range(KV_UNITS):
                if c < KV_SLABS * B:
                    ssq_k(c)
                if 0 <= c - 1 < KV_SLABS * B:
                    norm_k(c - 1)
                if c < B:
                    layer_stats(c, c)
                if 0 <= c - 21 < B:
                    turn_x_lo(c - 21, c - 21)
                if 0 <= c - 18 < B:
                    layer_norm(c - 18, c - 18)
                lo, hi = spread(0, Q0 * BOUNDS, KV_UNITS)[c]
                for t in range(lo, hi):
                    chain(t // BOUNDS, cols_of(t // BOUNDS), t % BOUNDS, t % BOUNDS + 1)
                    if t % BOUNDS == 10:
                        q = t // BOUNDS + 1
                        nf_prep(q, q % 3, cols_of(q))

            def step(g, s):
                parts = spread(SIGNS[s][1], SIGNS[s][2], 3)
                q = Q0 + 3 * g + SIGNS[s][0]
                mine = not isinstance(g, int) or g < G

                _, _, n = at(g, s, 1)
                if live(n):
                    dve.wait_ge(q_squared, n + 1)
                    wait(dve, q_rq, n - 3)
                    dve.tensor_reduce(ssq[:, (s - 1) % 4, :], heads(sq_sb[:, :]), AX.X, ALU.add).then_inc(q_ssq, 1)
                if mine:
                    chain(q, QC, *parts[0])

                _, _, n = at(g, s, 2)
                if live(n):
                    r = n_par(s, 2)
                    dve.wait_ge(p_exp, n + 1)
                    dve.reciprocal(rsum[:, r, :], psum_[:, r, :]).then_inc(p_rsum, 1)

                _, b, n = at(g, s, 4)
                if live(n):
                    dve.wait_ge(attn_ready, n + 1)
                    wait(dve, attn_added, n)
                    dve.tensor_tensor(resid[:, b, :], resid[:, b, :], attn_ps[:, :], ALU.add).then_inc(attn_added, 1)
                if mine:
                    chain(q, QC, *parts[1])

                _, _, n = at(g, s, 3)
                if live(n):
                    r = n_par(s, 3)
                    dve.wait_ge(oT_hi, n + 1)
                    dve.tensor_tensor(o_lo_sb[:, r, :], oT_ps[:, :], o_hi_sb[:, r, :], ALU.subtract).then_inc(oT_lo, 1)

                _, _, n = at(g, s, 1)
                if live(n):
                    r = n_par(s, 1)
                    dve.wait_ge(s_ready, n + 1)
                    dve.wait_ge(q_rq, n + 1)
                    wait(dve, p_exp, n - 1)
                    if isinstance(n, int) and n == 0:
                        dve.wait_ge(mask_in, 16)
                    for j in range(J):
                        ins = dve.scalar_tensor_tensor(s_sb[:, r, j * S:(j + 1) * S], s_ps[r][:, j * S:(j + 1) * S],
                                                       rq[:, (s - 1) % 4, j:j + 1], mask_sb[:, :],
                                                       op0=ALU.mult, op1=ALU.add)
                    ins.then_inc(s_scaled, 1)
                    dve.wait_ge(s_scaled, n + 1)
                    dve.tensor_reduce(nmax[:, r, :], heads(s_sb[:, r, :]), AX.X, ALU.max, negate=True).then_inc(s_max, 1)

                if mine:
                    chain(q, QC, *parts[2])
                    if s in (1, 4):
                        nf_prep(q + 1, SIGNS[s][0] + 1, QC)
                    if s == 6 and not (isinstance(g, int) and g == G - 1):
                        nf_prep(q + 1, 0, QC)

            for s in range(B):
                step(0, s)
            with dve.Fori(1, G - 1) as g:
                for s in range(B):
                    step(g, s)
            for s in range(B):
                step(G - 1, s)
            for s in range(4):
                step(G, s)

            dve.wait_ge(attn_added, N)
            for b in range(B):
                layer_stats(B + b, b)
            for b in range(B):
                layer_norm(B + b, b)
                if b >= 1:
                    turn_x_lo(B + b - 1, b - 1)
            turn_x_lo(2 * B - 1, B - 1)

            def split_w(t, par, M, parts):
                for c in parts:
                    u = 3 * t + c
                    dve.wait_ge(w_hi, u + 1)
                    bank = wT_ps[(3 * par + c) % 2]
                    if c < 2:
                        dve.tensor_tensor(wT_part(par, c, 1, M), bank[:, 0:KT * M].rearrange("p (k m) -> p k m", k=KT),
                                          wT_part(par, c, 0, M), ALU.subtract).then_inc(w_lo, 1)
                    else:
                        dve.tensor_tensor(w3_part(par, 1, M), bank[0:M, :], w3_part(par, 0, M), ALU.subtract)\
                            .then_inc(w_lo, 1)

            def hidden(t, par, M, half):
                v = 2 * t + half
                dve.wait_ge(silu_done, v + 1)
                dve.wait_ge(up_ready, v + 1)
                wait(dve, h_lo, v - 1)
                dve.tensor_tensor(h_sb[0:M, half, :], s_ps[half][0:M, :], silu_sb[0:M, half, :], ALU.mult).then_inc(h_done, 1)
                dve.wait_ge(h_hi, v + 1)
                dve.tensor_tensor(hT_lo[0:M, par, half * 512:(half + 1) * 512], h_sb[0:M, half, :],
                                  hT_hi[0:M, par, half * 512:(half + 1) * 512], ALU.subtract).then_inc(h_lo, 1)

            def add_down(t, m):
                dve.wait_ge(down_ready, B * t + m + 1)
                wait(dve, down_added, B * t + m)
                dve.tensor_tensor(resid[:, m, :], resid[:, m, :], down_ps[m % 2][:, :], ALU.add).then_inc(down_added, 1)

            def ffn(t, par):
                if has_tile(t - 1):
                    split_w(t - 1, 1 - par, rows_of(t - 1), [2])
                if has_tile(t):
                    split_w(t, par, rows_of(t), [0, 1])
                for half in range(2):
                    if has_tile(t - 1):
                        hidden(t - 1, 1 - par, rows_of(t - 1), half)
                    if has_tile(t - 2):
                        for m in range(4 * half, 4 * half + 4):
                            add_down(t - 2, m)

            for t in range(4):
                ffn(t, t % 2)
            with dve.Fori(2, FT // 2) as tt:
                for par in range(2):
                    ffn(tt * 2 + par, par)
            for t in range(FT, TILES + 2):
                ffn(t, t % 2)

        @block.gpsimd
        def _(pool):
            def low_part(dst, src, hi):
                return pool.tensor_tensor(dst, src, hi, ALU.subtract)

            def slab_part(m, k, dst):
                pool.wait_ge(slab_hi, KT * m + k + 1)
                low_part(dst[:, 1, k, :], raw[:, k, :], dst[:, 0, k, :]).then_inc(slab_lo, 1)

            def nf_norm(q, cols):
                nb = cols // BLK
                pool.wait_ge(nf_rmax, q + 1)
                wait(pool, nf_signed, BOUNDS * q)
                pool.tensor_tensor(nf_n[:, 0:cols].rearrange("p (b e) -> p b e", e=BLK),
                                   nf_raw[:, 0:cols].rearrange("p (b e) -> p b e", e=BLK),
                                   rmax[:, 0:nb].unsqueeze(2).to_broadcast([P, nb, BLK]), ALU.mult).then_inc(nf_normed, 1)

            def nf_scale(q, slot, cols):
                nb = cols // BLK
                pool.wait_ge(nf_chained, BOUNDS * (q + 1))
                wait(pool, nf_out, 16 * q)
                pool.tensor_tensor(nf_dq[:, 0:cols], nf_pos[:, 0:cols], nf_neg[:, 0:cols], ALU.add).then_inc(nf_summed, 1)
                pool.wait_ge(nf_summed, q + 1)
                v = nf_dq[:, 0:cols].rearrange("p (b e) -> p b e", e=BLK)
                pool.tensor_tensor(v, v, safe[:, slot, 0:nb].unsqueeze(2).to_broadcast([P, nb, BLK]), ALU.mult)\
                    .then_inc(nf_scaled, 1)

            pool.memset(ident[:, :], 0.0).then_inc(const_zero, 1)
            pool.memset(neg_half[:, :], -0.5).then_inc(const_set, 1)
            pool.memset(hd_eps[:, :], HD * EPS).then_inc(const_set, 1)
            pool.wait_ge(const_zero, 1)
            pool.affine_select(out=ident[:, :], in_=ident[:, :], compare_op=ALU.not_equal, fill=1.0, base=0,
                               pattern=[[-1, P]], channel_multiplier=1).then_inc(const_done, 1)
            pool.wait_ge(const_set, 2)

            for k in range(KT):
                slab_part(0, k, slab_slot(0))
            nf_norm(0, cols_of(0))
            for k in range(KT):
                slab_part(1, k, slab_slot(1))

            def rms(n, slot, ssq_sem, var_sem, out_sem):
                pool.wait_ge(ssq_sem, n + 1)
                wait(pool, out_sem, n)
                pool.tensor_tensor(var[:, :], ssq[:, slot, :], hd_eps[:, :], ALU.add).then_inc(var_sem, 1)
                pool.wait_ge(var_sem, n + 1)
                pool.tensor_tensor(rq[:, slot, :], var[:, :], neg_half[:, 0:J], ALU.pow).then_inc(out_sem, 1)

            def ln_scale(count):
                pool.wait_ge(ln_mv, B * count)
                pool.tensor_scalar(ln_var_sb[:, :], mv[:, :, 1], 1.0, LN_EPS, ALU.mult, ALU.add).then_inc(ln_var, 1)
                pool.wait_ge(ln_var, count)
                pool.tensor_tensor(rstd[:, :], ln_var_sb[:, :], neg_half[:, 0:B], ALU.pow).then_inc(ln_rstd, 1)

            for c in range(KV_UNITS):
                m, b, is_k = kv_kind(c)
                if is_k:
                    wait(pool, k_normed, c - 3)
                    rms(c, c % 4, kv_ssq, kv_var, kv_rk)
                if c == 12:
                    ln_scale(1)
                if m >= 1 and m < 4 and b < KT:
                    slab_part(m + 1, b, slab_slot(m + 1))
                lo, hi = spread(0, Q0 * BOUNDS, KV_UNITS)[c]
                for t in range(lo, hi):
                    if t % BOUNDS == BOUNDS - 1:
                        q = t // BOUNDS
                        nf_norm(q + 1, cols_of(q + 1))
                        nf_scale(q, q % 3, cols_of(q))

            def step(g, s):
                q = Q0 + 3 * g + SIGNS[s][0]
                mine = not isinstance(g, int) or g < G
                last = isinstance(g, int) and g == G - 1
                _, _, n = at(g, s, 1)
                if live(n):
                    wait(pool, s_scaled, n - 3)
                    rms(n, (s - 1) % 4, q_ssq, q_var, q_rq)
                _, _, n = at(g, s, 2)
                if live(n):
                    r = n_par(s, 2)
                    pool.wait_ge(p_rsum, n + 1)
                    v = heads(p_sb[:, r, :])
                    pool.tensor_tensor(v, v, rsum[:, r, :].unsqueeze(2).to_broadcast([P, J, S]), ALU.mult)\
                        .then_inc(p_normed, 1)
                if mine and s < KT and not last:
                    slab_part(2 * KV_SLABS + 1 + g, s, ring[:, (g + 1) % 2, :, :, :])
                if mine and s == 3:
                    for j in range(J):
                        pool.wait_ge(wo_hi_done, J * g + j + 1)
                        low_part(wo_lo[:, j, :], wo_raw[:, j, :], wo_hi[:, j, :]).then_inc(wo_lo_done, 1)
                if mine and s in (2, 5, 7):
                    if not (last and s == 7):
                        nf_norm(q + 1, QC)
                    nf_scale(q, SIGNS[s][0], QC)

            for s in range(B):
                step(0, s)
            with pool.Fori(1, G - 1) as g:
                for s in range(B):
                    step(g, s)
            for s in range(B):
                step(G - 1, s)
            for s in range(4):
                step(G, s)
            ln_scale(2)


_OUT = ((B, S, D), "float32")


def kernel(**inputs):
    import numpy as _np
    import concourse.bacc as _bacc
    from concourse import mybir as _mybir
    from concourse.bass_utils import run_bass_kernel_spmd as _run

    a = {k: _np.asarray(v) for k, v in inputs.items()}
    laid = {
        "x": a["x"],
        "ctxT": a["ctx_4096"].reshape(B * S, D).T,
        "mask": a["mask_1x1xSxS2_ff0"],
        "wqT": a["L0_xattn_q_proj_w"].T,
        "wkT": a["L0_xattn_k_proj_w"].T,
        "wvT": a["L0_xattn_v_proj_w"].T,
        "woT": a["L0_xattn_o_proj_w"].T,
        "qnw": a["L0_xattn_q_norm_w"],
        "knw": a["L0_xattn_k_norm_w"],
        "w1": a["L0_ffn_w1"].reshape(P, FLAT),
        "w2": a["L0_ffn_w2"].reshape(P, FLAT),
        "w3": a["L0_ffn_w3"].reshape(P, FLAT),
    }
    nc = _bacc.Bacc("TRN2", target_bir_lowering=False, num_devices=1)
    arrays, args = {}, []
    for name, v in laid.items():
        v = _np.ascontiguousarray(v)
        arrays[f"in_{name}"] = v
        args.append(nc.dram_tensor(f"in_{name}", v.shape, _mybir.dt.from_np(v.dtype), kind="ExternalInput").ap())
    out = nc.dram_tensor("out_0", _OUT[0], _mybir.dt.from_np(_np.dtype(_OUT[1])), kind="ExternalOutput").ap()
    build(nc, *args, out)
    r = _run(nc, [arrays], core_ids=[0])
    return r.results[0]["out_0"]
```

```python
import concourse.bass as bass
from concourse import mybir
from contextlib import ExitStack
import numpy as np

F32 = mybir.dt.float32
F32R = mybir.dt.float32r
BF16 = mybir.dt.bfloat16
ALU = mybir.AluOpType
ACT = mybir.ActivationFunctionType
AX = mybir.AxisListType

P = 128
B = 8
S = 128
D = 512
KT = D // P
HD = 128
G = 8
J = 4
N = G * B
F = 1376
FT = F // P
FR = F - FT * P
TILES = FT + 1
EPS = 1e-5
LN_EPS = 1e-5
GC = D // HD
KV_SLABS = G // GC
KV_UNITS = 2 * KV_SLABS * B

CODE = np.array([-1.0, -0.6961928009986877, -0.5250730514526367, -0.39491748809814453,
                 -0.28444138169288635, -0.18477343022823334, -0.09105003625154495, 0.0,
                 0.07958029955625534, 0.16093020141124725, 0.24611230194568634, 0.33791524171829224,
                 0.44070982933044434, 0.5626170039176941, 0.7229568362236023, 1.0], np.float32)
BOUND = ((CODE[:-1] + CODE[1:]) * np.float32(0.5)).astype(np.float32)
ZERO = 7
BOUNDS = len(BOUND)
BLK = 64
FLAT = F * D // P
QC = 512
QREST = FLAT - G * QC
EARLY = [512, 448, 448]
assert sum(EARLY) == QREST and all(n % BLK == 0 for n in EARLY)
Q0 = 3 * len(EARLY)
ORDER = [7, 0, 8, 1, 9, 2, 10, 3, 11, 4, 12, 5, 13, 6, 14]
RING = 5


def build(nc, x, ctxT, mask, wqT, wkT, wvT, woT, qnw, knw, w1, w2, w3, out):
    weights = [w1, w2, w3]
    dq_dram = [nc.dram_tensor(f"dq{j + 1}_scratch", [P, FLAT], F32).ap() for j in range(3)]
    v_dram = nc.dram_tensor("v_scratch", [G, P, B, HD], F32).ap()
    dq1 = dq_dram[0].rearrange("p n -> (p n)").rearrange("(h d) -> h d", d=D)
    dq2 = dq_dram[1].rearrange("p n -> (p n)").rearrange("(h d) -> h d", d=D)
    dq3 = dq_dram[2].rearrange("p n -> (p n)").rearrange("(r p h) -> p r h", r=KT, p=P)
    wq_v = wqT.rearrange("(k p) n -> p k n", p=P)
    wk_v = wkT.rearrange("(k p) n -> p k n", p=P)
    wv_v = wvT.rearrange("(k p) n -> p k n", p=P)
    wo_v = woT.rearrange("(h p) n -> p h n", p=P)
    ctx_v = ctxT.rearrange("(k p) n -> p k n", p=P)

    es = ExitStack()
    with es:
        def sb(name, shape, dt=F32):
            return es.enter_context(nc.sbuf_tensor(name, shape, dt))

        def ps(name):
            return es.enter_context(nc.psum_tensor(name, [P, 512], F32))

        def sem(name):
            return es.enter_context(nc.semaphore(name))

        resid = sb("resid", [P, B, D])
        xT_hi = sb("xT_hi", [P, KT, B * S], F32R)
        xT_lo = sb("xT_lo", [P, KT, B * S], F32R)
        early = sb("early", [P, 2 * KT * B * S], F32R)
        ctx_hi = early[:, 0:KT * B * S].rearrange("p (k n) -> p k n", k=KT)
        ctx_lo = early[:, KT * B * S:].rearrange("p (k n) -> p k n", k=KT)
        wo_sb = early[:, 0:6144].rearrange("p (j l n) -> p j l n", j=6, l=2)
        o_hi_sb = early[:, 6144:7168].rearrange("p (r n) -> p r n", r=2)
        o_lo_sb = early[:, 7168:8192].rearrange("p (r n) -> p r n", r=2)
        hT_hi = early[:, 0:2048].rearrange("p (r n) -> p r n", r=2)
        hT_lo = early[:, 2048:4096].rearrange("p (r n) -> p r n", r=2)
        kT = sb("kT", [P, G, B * S])
        ring = sb("ring", [P, 2, 2, KT, 512], F32R)
        wT = ring[:, :, :, :, :].rearrange("p s l k n -> p s (l k n)")
        raw = sb("raw", [P, KT, 512])
        wo_raw = sb("wo_raw", [P, J, 512])
        v_sb = sb("v_sb", [P, B, HD])
        wqk = sb("wqk", [P, 1])
        qn_sb = sb("qn_sb", [P, 1])
        kn_sb = sb("kn_sb", [P, 1])
        mask_sb = sb("mask_sb", [P, S])
        ident = sb("ident", [P, P])
        neg_half = sb("neg_half", [P, B])
        hd_eps = sb("hd_eps", [P, J])
        ln_eps = sb("ln_eps", [P, 4])
        q_sb = sb("q_sb", [P, 2, 512])
        sq_sb = sb("sq_sb", [P, 512])
        qT_sb = sb("qT_sb", [P, 2, 512])
        sp_sb = sb("sp_sb", [P, 4, 512])
        s_sb = sp_sb[:, 0:2, :]
        p_sb = sp_sb[:, 2:4, :]
        pT_sb = sb("pT_sb", [P, 2, 512])
        ctx_raw = [wo_raw[:, :, :], sp_sb[:, :, :]]
        ssq = sb("ssq", [P, 4, J])
        var = sb("var", [P, J])
        ln_var_sb = sb("ln_var_sb", [P, B])
        rq = sb("rq", [P, 4, J])
        nmax = sb("nmax", [P, 2, J])
        psum_ = sb("psum_", [P, 2, J])
        rsum = sb("rsum", [P, 2, J])
        stats = sb("stats", [P, B, 6])
        mv = sb("mv", [P, B, 2])
        rstd = sb("rstd", [P, B])
        nf_raw = sb("nf_raw", [P, QC])
        nf_n = sb("nf_n", [P, 3, QC])
        nf_sign = sb("nf_sign", [P, RING, QC], BF16)
        nf_pos = sb("nf_pos", [P, QC])
        nf_neg = sb("nf_neg", [P, QC])
        nf_dq = sb("nf_dq", [P, QC])
        amax = sb("amax", [P, QC // BLK])
        safe = sb("safe", [P, 3, QC // BLK])
        rmax = sb("rmax", [P, QC // BLK])
        wn = kT[:, :, :].rearrange("p g n -> p (g n)")[:, 0:2 * 1536].rearrange("p (s c n) -> p s c n", s=2, c=3)
        silu_sb = s_sb
        h_sb = p_sb

        proj_ps = [ps("proj_ps0"), ps("proj_ps1")]
        turn_ps = ps("turn_ps")
        s_ps = [ps("s_ps0"), ps("s_ps1")]
        pT_ps = ps("pT_ps")
        oT_ps = ps("oT_ps")
        attn_ps = ps("attn_ps")

        x_in, small_in, mask_in = sem("x_in"), sem("small_in"), sem("mask_in")
        ctx_in = [sem(f"ctx_in{k}") for k in range(KT + 1)]
        raw_in = [sem(f"raw_in{k}") for k in range(KT)]
        wo_in = [sem(f"wo_in{j}") for j in range(J)]
        v_in = [sem("v_in0"), sem("v_in1")]
        v_out = [sem("v_out0"), sem("v_out1")]
        nf_in, nf_out = sem("nf_in"), sem("nf_out")
        wn_in = [sem("wn_in0"), sem("wn_in1")]
        y_out = sem("y_out")
        const_zero, const_set, const_done, wqk_done = (sem(n) for n in ("const_zero", "const_set", "const_done", "wqk_done"))
        ctx_hi_done, ctx_lo_done = sem("ctx_hi_done"), sem("ctx_lo_done")
        slab_hi, slab_lo = sem("slab_hi"), sem("slab_lo")
        wo_hi_done, wo_lo_done = sem("wo_hi_done"), sem("wo_lo_done")
        kv_ready, kv_squared, kv_ssq, kv_var, kv_rk = (sem(n) for n in ("kv_ready", "kv_squared", "kv_ssq", "kv_var", "kv_rk"))
        k_normed, k_turned, k_stored, v_copied = (sem(n) for n in ("k_normed", "k_turned", "k_stored", "v_copied"))
        ln_stats, ln_mv, ln_var, ln_rstd, ln_x, ln_turned, ln_hi, ln_lo = (
            sem(n) for n in ("ln_stats", "ln_mv", "ln_var", "ln_rstd", "ln_x", "ln_turned", "ln_hi", "ln_lo"))
        q_ready, q_copied, q_squared, q_ssq, q_var, q_rq = (
            sem(n) for n in ("q_ready", "q_copied", "q_squared", "q_ssq", "q_var", "q_rq"))
        qT_ready, qT_copied, s_ready, s_scaled, s_max, p_exp, p_rsum, p_normed = (
            sem(n) for n in ("qT_ready", "qT_copied", "s_ready", "s_scaled", "s_max", "p_exp", "p_rsum", "p_normed"))
        pT_ready, pT_copied, oT_ready, oT_hi, oT_lo, attn_ready, attn_added = (
            sem(n) for n in ("pT_ready", "pT_copied", "oT_ready", "oT_hi", "oT_lo", "attn_ready", "attn_added"))
        nf_amax, nf_safe, nf_rmax, nf_normed, nf_signed, nf_chained, nf_summed, nf_scaled = (
            sem(n) for n in ("nf_amax", "nf_safe", "nf_rmax", "nf_normed", "nf_signed", "nf_chained", "nf_summed", "nf_scaled"))
        w_turned, w_hi, w_lo, gate_ready, up_ready, silu_done, h_done, h_hi, h_lo, down_ready, down_added = (
            sem(n) for n in ("w_turned", "w_hi", "w_lo", "gate_ready", "up_ready", "silu_done", "h_done",
                             "h_hi", "h_lo", "down_ready", "down_added"))
        block = es.enter_context(nc.Block())

        def wait(eng, s, count):
            if not isinstance(count, int) or count > 0:
                eng.wait_ge(s, count)

        def live(n):
            return not isinstance(n, int) or 0 <= n < N

        def wo_part(l, g, j):
            return wo_sb[:, 2 + j, l, :] if j >= 2 else wo_sb[:, (g % 2) * 2 + j, l, :]

        def slab_slot(m):
            return ring[:, m % 2, :, :, :]

        def heads(ap):
            return ap.rearrange("p (j n) -> p j n", j=J)

        def kv_kind(c):
            return c // B, c % B, c < KV_SLABS * B

        kv_ps = [proj_ps[0], proj_ps[1], s_ps[0], s_ps[1]]
        wT_ps = [turn_ps, pT_ps]
        down_ps = [oT_ps, attn_ps]

        def x_ps(n):
            return turn_ps if B <= n < B + 4 else (oT_ps, attn_ps)[n % 2]

        def n_par(s, lag):
            return (s - lag) % 2

        def has_tile(t):
            return not isinstance(t, int) or 0 <= t < TILES

        def rows_of(t):
            return FR if isinstance(t, int) and t == TILES - 1 else P

        def wT_part(par, c, l, M):
            at = 2048 * l + 512 * c
            return wT[:, par, at:at + KT * M].rearrange("p (k m) -> p k m", k=KT)

        def w3_part(par, l, M):
            at = 2048 * l + 1024
            return wT[0:M, par, at:at + D]

        def WN_COUNT(t):
            return 48 * (t // 2 + 1)

        def chunk_ap(tensors, g, j):
            return tensors[j][:, bass.ds(g * QC, QC)] if not isinstance(g, int) else tensors[j][:, g * QC:(g + 1) * QC]

        def early_ap(tensors, q):
            j, e = divmod(q, len(EARLY))
            at = G * QC + sum(EARLY[:e])
            return tensors[j][:, at:at + EARLY[e]]

        def cols_of(q):
            return EARLY[q % len(EARLY)] if q < Q0 else QC

        WO_STEP = {0: [0], 1: [1], 3: [2, 3]}
        CUTS = [0, 2, 4, 6, 8, 10, 12, 14, 15, 17, 19, 21, 22, 24, 26, 28, 29, 30, 33, 35, 37, 39, 41, 43, 45]
        LEAD = 3

        def bounds_in(g, s, part, lead):
            if isinstance(g, int) and g >= G:
                return []
            lo, hi = (CUTS[3 * s + part + i] + lead for i in range(2))
            end = 3 * BOUNDS if isinstance(g, int) and g == G - 1 else hi
            lo = 0 if isinstance(g, int) and g == s == part == 0 else lo
            return [divmod(n, BOUNDS) for n in range(lo, min(hi, end))]

        def spread(lo, hi, parts):
            cut = [lo + (hi - lo) * i // parts for i in range(parts + 1)]
            return list(zip(cut[:-1], cut[1:]))

        @block.sync
        def _(sp):
            def load_slab(m, src):
                for k in range(KT):
                    wait(sp, slab_lo, (m - 1) * KT + k + 1)
                    sp.dma_start(raw[:, k, :], src[:, k, :]).then_inc(raw_in[k], 16)

            def load_wo(g):
                for j in range(J):
                    wait(sp, wo_lo_done, (g - 1) * J + j + 1)
                    sp.dma_start(wo_raw[:, j, :], wo_v[:, g * J + j, :]).then_inc(wo_in[j], 16)

            def load_v(g, half):
                wait(sp, oT_ready, g * B - (4 if half == 0 else 0))
                sp.dma_start(v_sb[:, 4 * half:4 * half + 4, :], v_dram[g, :, 4 * half:4 * half + 4, :])\
                    .then_inc(v_in[half], 16)

            def nf_load(q, src, cols):
                wait(sp, nf_normed, q)
                sp.dma_start(nf_raw[:, 0:cols], src).then_inc(nf_in, 16)

            def nf_store(q, dst, cols):
                wait(sp, nf_scaled, q + 1)
                sp.dma_start(dst, nf_dq[:, 0:cols]).then_inc(nf_out, 16)

            kv_src = [wk_v[:, :, 0:512], wk_v[:, :, 512:1024], wv_v[:, :, 0:512], wv_v[:, :, 512:1024]]
            for k in range(KT):
                sp.dma_start(ctx_raw[0][:, k, :], ctx_v[:, k, 0:512]).then_inc(ctx_in[k], 16)
                sp.dma_start(raw[:, k, :], kv_src[0][:, k, :]).then_inc(raw_in[k], 16)
            def nf_early(q):
                nf_load(q, early_ap(weights, q) if q < Q0 else chunk_ap(weights, 0, 0), cols_of(q))
                if q >= 2:
                    nf_store(q - 2, early_ap(dq_dram, q - 2), cols_of(q - 2))

            nf_early(0)
            sp.dma_start(ctx_raw[1], ctx_v[:, :, 512:1024]).then_inc(ctx_in[KT], 16)
            load_slab(1, kv_src[1])
            sp.dma_start(resid[:, :, :], x.rearrange("b s d -> s b d")).then_inc(x_in, 16)
            sp.dma_start(qn_sb[:, :], qnw.rearrange("(p a) -> p a", a=1)).then_inc(small_in, 16)
            sp.dma_start(kn_sb[:, :], knw.rearrange("(p a) -> p a", a=1)).then_inc(small_in, 16)
            sp.dma_start(mask_sb[:, :], mask[0, 0, :, :]).then_inc(mask_in, 16)
            nf_early(1)
            load_slab(2, kv_src[2])
            for q in range(2, Q0 + 1):
                nf_early(q)
                if q == 3:
                    load_slab(3, kv_src[3])
                if q == 5:
                    load_slab(4, wq_v[:, :, 0:512])
            sp.wait_ge(ctx_lo_done, 2 * KT)
            for p in range(2):
                sp.wait_ge(v_out[p], 16 * KV_SLABS * B // 2)

            def body(g, last):
                q = Q0 + 3 * g
                nf_load(q + 1, chunk_ap(weights, g, 1), QC)
                load_v(g, 0)
                load_wo(g)
                if not last:
                    load_slab(5 + g, wq_v[:, :, bass.ds((g + 1) * 512, 512)])
                if isinstance(g, int) and g == 0:
                    nf_store(q - 1, early_ap(dq_dram, Q0 - 1), cols_of(Q0 - 1))
                else:
                    nf_store(q - 1, chunk_ap(dq_dram, g - 1, 2), QC)
                load_v(g, 1)
                nf_load(q + 2, chunk_ap(weights, g, 2), QC)
                nf_store(q, chunk_ap(dq_dram, g, 0), QC)
                if not last:
                    nf_load(q + 3, chunk_ap(weights, g + 1, 0), QC)
                nf_store(q + 1, chunk_ap(dq_dram, g, 1), QC)

            body(0, False)
            with sp.Fori(1, G - 1) as g:
                body(g, False)
            body(G - 1, True)
            nf_store(Q0 + 3 * G - 1, chunk_ap(dq_dram, G - 1, 2), QC)

            sp.wait_ge(nf_out, 16 * (Q0 + 3 * G))
            sp.wait_ge(s_ready, N)

            def load_tile(t, par, M):
                wait(sp, w_turned, 3 * (t - 1))
                rows = bass.ds(t * P, M)
                sp.dma_start(wn[0:M, par, 0, :], dq1[rows, :]).then_inc(wn_in[par], 16)
                sp.dma_start(wn[0:M, par, 1, :], dq2[rows, :]).then_inc(wn_in[par], 16)
                sp.dma_start(wn[:, par, 2, 0:KT * M].rearrange("p (r m) -> p r m", r=KT), dq3[:, :, rows])\
                    .then_inc(wn_in[par], 16)

            for t in range(2):
                load_tile(t, t, P)
            with sp.Fori(1, FT // 2) as tt:
                for par in range(2):
                    load_tile(tt * 2 + par, par, P)
            load_tile(TILES - 1, (TILES - 1) % 2, FR)
            for m in range(B):
                sp.wait_ge(down_added, (TILES - 1) * B + m + 1)
                sp.dma_start(out[m, :, :], resid[:, m, :]).then_inc(y_out, 16)
            sp.wait_ge(y_out, 16 * B)

        def at(g, s, lag):
            return g + (s - lag) // B, (s - lag) % B, B * g + s - lag

        @block.tensor
        def _(pe):
            def turn(bank, src, cols, rows=P):
                for k in range(len(src)):
                    mm = pe.transpose(bank[0:cols, k * rows:(k + 1) * rows], src[k], ident[0:rows, 0:rows])
                return mm

            def three_pass(bank, pairs):
                for n, (a_hi, a_lo, b_hi, b_lo) in enumerate(pairs):
                    pe.matmul(bank, a_hi, b_hi, start=(n == 0), stop=False)
                    pe.matmul(bank, a_hi, b_lo, start=False, stop=False)
                    mm = pe.matmul(bank, a_lo, b_hi, start=False, stop=(n == len(pairs) - 1))
                return mm

            def tokens(ap, k, b):
                return ap[:, k, b * S:(b + 1) * S]

            def kv(c):
                m, b, _ = kv_kind(c)
                pe.wait_ge(slab_lo, KT * (m + 1))
                pe.wait_ge(ctx_lo_done, KT * (b // 4 + 1))
                if 4 <= c < KV_SLABS * B + 4:
                    pe.wait_ge(k_normed, c - 3)
                elif c >= 4:
                    pe.wait_ge(v_copied, c - 3 - KV_SLABS * B)
                three_pass(kv_ps[c % 4][:, :], [
                    (tokens(ctx_hi, k, b), tokens(ctx_lo, k, b), slab_slot(m)[:, 0, k, :], slab_slot(m)[:, 1, k, :])
                    for k in range(KT)]).then_inc(kv_ready, 1)

            def turn_k(c):
                pe.wait_ge(k_normed, c + 1)
                wait(pe, k_stored, c)
                turn(turn_ps, [q_sb[:, c % 2, j * HD:(j + 1) * HD] for j in range(J)], P).then_inc(k_turned, 1)

            def turn_x(n):
                pe.wait_ge(ln_x, n + 1)
                if n == B:
                    pe.wait_ge(qT_copied, N)
                elif n == B + 4:
                    pe.wait_ge(oT_lo, N)
                elif n == B + 5:
                    pe.wait_ge(attn_added, N)
                wait(pe, ln_lo, n if B < n < B + 4 else n - 1)
                turn(x_ps(n), [qT_sb[:, n % 2, k * P:(k + 1) * P] for k in range(KT)], P).then_inc(ln_turned, 1)

            pe.wait_ge(const_done, 1)
            for c in range(KV_UNITS):
                kv(c)
                if 0 <= c - 3 < KV_SLABS * B:
                    turn_k(c - 3)
                if 0 <= c - 20 < B:
                    turn_x(c - 20)

            def step(g, s):
                _, _, n = at(g, s, 3)
                if live(n):
                    pe.wait_ge(p_normed, n + 1)
                    wait(pe, pT_copied, n)
                    turn(pT_ps, [p_sb[:, n_par(s, 3), j * S:(j + 1) * S] for j in range(J)], P).then_inc(pT_ready, 1)

                def project(heads_of):
                    gg, _, n = at(g, s, 4)
                    if not live(n):
                        return
                    if heads_of[0] == 0:
                        pe.wait_ge(oT_lo, n + 1)
                        wait(pe, attn_added, n)
                        if isinstance(n, int) and n == 0:
                            pe.wait_ge(ln_lo, B)
                    for j in heads_of:
                        pe.wait_ge(wo_lo_done, gg * J + j + 1)
                        r = n_par(s, 4)
                        oh, ol = (t[:, r, j * S:(j + 1) * S] for t in (o_hi_sb, o_lo_sb))
                        w_hi_, w_lo_ = (wo_part(l, gg, j) for l in range(2))
                        pe.matmul(attn_ps[:, :], oh, w_hi_, start=(j == 0), stop=False)
                        pe.matmul(attn_ps[:, :], oh, w_lo_, start=False, stop=False)
                        mm = pe.matmul(attn_ps[:, :], ol, w_hi_, start=False, stop=(j == J - 1))
                    if heads_of[-1] == J - 1:
                        mm.then_inc(attn_ready, 1)

                project([0, 1])

                _, _, n = at(g, s, 1)
                if live(n):
                    pe.wait_ge(q_copied, n + 1)
                    wait(pe, qT_copied, n)
                    if isinstance(n, int) and n == 0:
                        pe.wait_ge(k_stored, KV_SLABS * B)
                    turn(turn_ps, [q_sb[:, n_par(s, 1), j * HD:(j + 1) * HD] for j in range(J)], P).then_inc(qT_ready, 1)

                project([2, 3])

                gg, b, n = at(g, s, 3)
                if live(n):
                    pe.wait_ge(pT_copied, n + 1)
                    pe.wait_ge(v_in[b // 4], 16 * (gg + 1))
                    wait(pe, oT_lo, n)
                    if isinstance(n, int) and n == 0:
                        pe.wait_ge(ln_lo, B)
                    pe.matmul(oT_ps[:, :], v_sb[:, b, :], pT_sb[:, n_par(s, 3), :], start=True, stop=True)\
                        .then_inc(oT_ready, 1)

                gg, b, n = at(g, s, 1)
                if live(n):
                    pe.wait_ge(qT_copied, n + 1)
                    wait(pe, s_scaled, n - 1)
                    if isinstance(n, int) and n == 0:
                        pe.wait_ge(k_stored, KV_SLABS * B)
                    for j in range(J):
                        mm = pe.matmul(s_ps[n_par(s, 1)][:, j * S:(j + 1) * S],
                                       qT_sb[:, n_par(s, 1), j * S:(j + 1) * S],
                                       kT[:, gg, b * S:(b + 1) * S], start=True, stop=True)
                    mm.then_inc(s_ready, 1)

                gg, b, n = at(g, s, 0)
                if live(n):
                    pe.wait_ge(slab_lo, KT * (2 * KV_SLABS + gg + 1))
                    wait(pe, q_squared, n - 1)
                    if isinstance(n, int) and n < 2:
                        pe.wait_ge(v_copied, KV_SLABS * B)
                    if isinstance(n, int) and n < B:
                        pe.wait_ge(ln_lo, n + 1)
                    slab = ring[:, gg % 2, :, :, :]
                    three_pass(proj_ps[n_par(s, 0)][:, :], [
                        (tokens(xT_hi, k, b), tokens(xT_lo, k, b), slab[:, 0, k, :], slab[:, 1, k, :])
                        for k in range(KT)]).then_inc(q_ready, 1)

            for s in range(B):
                step(0, s)
            with pe.Fori(1, G) as g:
                for s in range(B):
                    step(g, s)
            for s in range(4):
                step(G, s)
                if s >= 2:
                    turn_x(B + 2 * (s - 2))
                    turn_x(B + 2 * (s - 2) + 1)

            def turn_w(t, par, M, parts):
                pe.wait_ge(wn_in[par], WN_COUNT(t))
                for c in parts:
                    u = 3 * t + c
                    wait(pe, w_lo, u - 1)
                    if isinstance(t, int) and t == 0 and c == 0:
                        pe.wait_ge(ln_lo, B + 4)
                    if isinstance(t, int) and t == 0 and c == 1:
                        pe.wait_ge(pT_copied, N)
                    bank = wT_ps[(3 * par + c) % 2]
                    if c < 2:
                        mm = turn(bank, [wn[0:M, par, c, k * P:(k + 1) * P] for k in range(KT)], P, M)
                    else:
                        mm = turn(bank, [wn[:, par, 2, r * M:(r + 1) * M] for r in range(KT)], M, P)
                    mm.then_inc(w_turned, 1)

            def product(bank, t, par, M, c, half, ready):
                pe.wait_ge(w_lo, 3 * t + c + 1)
                if isinstance(t, int) and t == 0:
                    pe.wait_ge(ln_lo, B + 4 * (half + 1))
                three_pass(bank[0:M, :], [
                    (wT_part(par, c, 0, M)[:, k, :], wT_part(par, c, 1, M)[:, k, :],
                     xT_hi[:, k, half * 512:(half + 1) * 512], xT_lo[:, k, half * 512:(half + 1) * 512])
                    for k in range(KT)]).then_inc(ready, 1)

            def gate(t, par, M, half):
                wait(pe, silu_done, 2 * t + half - 1)
                product(proj_ps[half], t, par, M, 0, half, gate_ready)

            def up(t, par, M, half):
                wait(pe, h_done, 2 * t + half - 1)
                product(s_ps[half], t, par, M, 1, half, up_ready)

            def down(t, par, M, m):
                pe.wait_ge(h_lo, 2 * t + m // 4 + 1)
                pe.wait_ge(w_lo, 3 * t + 3)
                wait(pe, down_added, B * t + m - 1)
                if isinstance(t, int) and t == 0 and m < 2:
                    pe.wait_ge(ln_lo, 2 * B)
                hh, hl = (a[0:M, par, m * S:(m + 1) * S] for a in (hT_hi, hT_lo))
                three_pass(down_ps[m % 2][:, :], [(hh, hl, w3_part(par, 0, M), w3_part(par, 1, M))])\
                    .then_inc(down_ready, 1)

            def ffn(t, par):
                if has_tile(t - 1):
                    turn_w(t - 1, 1 - par, rows_of(t - 1), [2])
                for half in range(2):
                    if has_tile(t - 1):
                        gate(t - 1, 1 - par, rows_of(t - 1), half)
                    if has_tile(t - 2):
                        for m in (4 * half, 4 * half + 1):
                            down(t - 2, par, rows_of(t - 2), m)
                    if has_tile(t):
                        turn_w(t, par, rows_of(t), [half])
                    if has_tile(t - 1):
                        up(t - 1, 1 - par, rows_of(t - 1), half)
                    if has_tile(t - 2):
                        for m in (4 * half + 2, 4 * half + 3):
                            down(t - 2, par, rows_of(t - 2), m)
                    if isinstance(t, int) and t == 1 and half == 0:
                        for n in range(B + 4, 2 * B):
                            turn_x(n)

            for t in range(4):
                ffn(t, t % 2)
            with pe.Fori(2, FT // 2) as tt:
                for par in range(2):
                    ffn(tt * 2 + par, par)
            for t in range(FT, TILES + 2):
                ffn(t, t % 2)

        @block.scalar
        def _(act):
            def sign(q, slot, cols, t):
                i = ORDER[t]
                edge = BOUND[i] if i >= ZERO else np.nextafter(BOUND[i], np.float32(1))
                act.wait_ge(nf_normed, q + 1)
                wait(act, nf_chained, BOUNDS * q + t - RING + 1)
                act.activation(nf_sign[:, t % RING, 0:cols], nf_n[:, slot, 0:cols], ACT.Sign, bias=-float(edge))\
                    .then_inc(nf_signed, 1)

            def slab_part(m, k, dst, free, count):
                act.wait_ge(raw_in[k], 16 * (m + 1))
                wait(act, free, count)
                act.activation(dst[:, 0, k, :], raw[:, k, :], ACT.Copy).then_inc(slab_hi, 1)

            def turn_x_hi(n, b):
                act.wait_ge(ln_turned, n + 1)
                act.activation(xT_hi[:, :, b * S:(b + 1) * S], heads(x_ps(n)[:, :]), ACT.Copy).then_inc(ln_hi, 1)

            for k in range(KT):
                act.wait_ge(ctx_in[k], 16)
                act.activation(ctx_hi[:, k, 0:512], ctx_raw[0][:, k, :], ACT.Copy).then_inc(ctx_hi_done, 1)
                slab_part(0, k, slab_slot(0), kv_ready, 0)
            act.wait_ge(ctx_in[KT], 16)
            for k in range(KT):
                act.activation(ctx_hi[:, k, 512:1024], ctx_raw[1][:, k, :], ACT.Copy).then_inc(ctx_hi_done, 1)
            for k in range(KT):
                slab_part(1, k, slab_slot(1), kv_ready, 0)

            def store_k(c):
                m, b, _ = kv_kind(c)
                act.wait_ge(k_turned, c + 1)
                act.wait_ge(wqk_done, 2)
                act.activation(kT[:, m * GC:(m + 1) * GC, b * S:(b + 1) * S], heads(turn_ps[:, :]), ACT.Copy,
                               scale=wqk[:, 0:1]).then_inc(k_stored, 1)

            for c in range(KV_UNITS):
                m, b, is_k = kv_kind(c)
                if m >= 1 and m < 4 and b < KT:
                    slab_part(m + 1, b, slab_slot(m + 1), kv_ready, B * m)
                if is_k:
                    act.wait_ge(kv_ready, c + 1)
                    wait(act, kv_ssq, c)
                    act.activation(sq_sb[:, :], kv_ps[c % 4][:, :], ACT.Square).then_inc(kv_squared, 1)
                else:
                    v = c - KV_SLABS * B
                    act.wait_ge(kv_ready, c + 1)
                    wait(act, v_out[v % 2], 16 * (v // 2))
                    act.activation(pT_sb[:, c % 2, :], kv_ps[c % 4][:, :], ACT.Copy).then_inc(v_copied, 1)
                    act.wait_ge(v_copied, v + 1)
                    h0 = (m - KV_SLABS) * GC
                    act.dma_start(v_dram[h0:h0 + GC, :, b, :].rearrange("g p d -> p g d"), heads(pT_sb[:, c % 2, :]))\
                        .then_inc(v_out[v % 2], 16)
                if 0 <= c - 4 < KV_SLABS * B:
                    store_k(c - 4)
                if 0 <= c - 21 < B:
                    turn_x_hi(c - 21, c - 21)
                lo, hi = spread(0, Q0 * BOUNDS, KV_UNITS)[c]
                for t in range(lo, hi):
                    sign(t // BOUNDS, t // BOUNDS % 3, cols_of(t // BOUNDS), t % BOUNDS)

            def step(g, s):
                def signs(part):
                    for c, t in bounds_in(g, s, part, LEAD):
                        sign(Q0 + 3 * g + c, c % 3, QC, t)

                _, _, n = at(g, s, 1)
                if live(n):
                    r = n_par(s, 1)
                    act.wait_ge(q_ready, n + 1)
                    wait(act, qT_ready, n - 1)
                    if isinstance(n, int) and n == 0:
                        act.wait_ge(k_turned, KV_SLABS * B)
                    act.activation(q_sb[:, r, :], proj_ps[r][:, :], ACT.Copy).then_inc(q_copied, 1)
                    wait(act, q_ssq, n)
                    act.activation(sq_sb[:, :], proj_ps[r][:, :], ACT.Square).then_inc(q_squared, 1)

                _, _, n = at(g, s, 3)
                if live(n):
                    act.wait_ge(pT_ready, n + 1)
                    wait(act, oT_ready, n - 1)
                    if isinstance(n, int) and n < 2:
                        act.wait_ge(v_out[n], 16 * KV_SLABS * B // 2)
                    act.activation(pT_sb[:, n_par(s, 3), :], pT_ps[:, :], ACT.Copy).then_inc(pT_copied, 1)

                _, _, n = at(g, s, 2)
                if live(n):
                    r = n_par(s, 2)
                    act.wait_ge(s_max, n + 1)
                    wait(act, pT_ready, n - 1)
                    for j in range(J):
                        e = act.activation(p_sb[:, r, j * S:(j + 1) * S], s_sb[:, r, j * S:(j + 1) * S], ACT.Exp,
                                           bias=nmax[:, r, j:j + 1], accum_out=psum_[:, r, j:j + 1])
                    e.then_inc(p_exp, 1)

                _, _, n = at(g, s, 1)
                if live(n):
                    act.wait_ge(qT_ready, n + 1)
                    wait(act, s_ready, n - 1)
                    act.activation(qT_sb[:, n_par(s, 1), :], turn_ps[:, :], ACT.Copy).then_inc(qT_copied, 1)

                signs(0)

                _, _, n = at(g, s, 3)
                if live(n):
                    act.wait_ge(oT_ready, n + 1)
                    wait(act, attn_ready, n - 1)
                    if isinstance(n, int) and n == 0:
                        act.wait_ge(kv_ready, KV_UNITS)
                    act.activation(o_hi_sb[:, n_par(s, 3), :], oT_ps[:, :], ACT.Copy).then_inc(oT_hi, 1)

                signs(1)
                signs(2)

            for s in range(B):
                step(0, s)
            with act.Fori(1, G - 1) as g:
                for s in range(B):
                    step(g, s)
            for s in range(B):
                step(G - 1, s)
            for s in range(4):
                step(G, s)
                if s >= 2:
                    turn_x_hi(B + 2 * (s - 2), 2 * (s - 2))
                    turn_x_hi(B + 2 * (s - 2) + 1, 2 * (s - 2) + 1)


            def split_w(t, par, M, parts):
                for c in parts:
                    u = 3 * t + c
                    act.wait_ge(w_turned, u + 1)
                    if c < 2:
                        wait(act, up_ready, 2 * (t - 1))
                        src = wT_ps[(3 * par + c) % 2][:, 0:KT * M].rearrange("p (k m) -> p k m", k=KT)
                        act.activation(wT_part(par, c, 0, M), src, ACT.Copy).then_inc(w_hi, 1)
                    else:
                        wait(act, down_ready, B * (t - 1))
                        act.activation(w3_part(par, 0, M), wT_ps[(3 * par + c) % 2][0:M, :], ACT.Copy).then_inc(w_hi, 1)

            def silu(t, M, half):
                v = 2 * t + half
                act.wait_ge(gate_ready, v + 1)
                wait(act, h_done, v - 1)
                act.activation(silu_sb[0:M, half, :], proj_ps[half][0:M, :], ACT.Silu).then_inc(silu_done, 1)

            def hidden_hi(t, par, M, half):
                v = 2 * t + half
                act.wait_ge(h_done, v + 1)
                wait(act, down_ready, B * (t - 1))
                act.activation(hT_hi[0:M, par, half * 512:(half + 1) * 512], h_sb[0:M, half, :], ACT.Copy)\
                    .then_inc(h_hi, 1)

            def ffn(t, par):
                if has_tile(t - 1):
                    split_w(t - 1, 1 - par, rows_of(t - 1), [2])
                for half in range(2):
                    if has_tile(t - 1):
                        silu(t - 1, rows_of(t - 1), half)
                    if has_tile(t):
                        split_w(t, par, rows_of(t), [half])
                    if isinstance(t, int) and t == 1 and half == 0:
                        for b in range(4, B):
                            turn_x_hi(B + b, b)
                    if has_tile(t - 1):
                        hidden_hi(t - 1, 1 - par, rows_of(t - 1), half)

            for t in range(4):
                ffn(t, t % 2)
            with act.Fori(2, FT // 2) as tt:
                for par in range(2):
                    ffn(tt * 2 + par, par)
            for t in range(FT, TILES + 1):
                ffn(t, t % 2)

        @block.vector
        def _(dve):
            def nf_prep(q, slot, cols):
                nb = cols // BLK
                dve.wait_ge(nf_in, 16 * (q + 1))
                wait(dve, nf_scaled, q - 2)
                dve.tensor_reduce(amax[:, 0:nb], nf_raw[:, 0:cols].rearrange("p (b e) -> p b e", e=BLK),
                                  AX.X, ALU.max, apply_absolute_value=True).then_inc(nf_amax, 1)
                dve.wait_ge(nf_amax, q + 1)
                dve.scalar_tensor_tensor(safe[:, slot, 0:nb], amax[:, 0:nb], 0.0, amax[:, 0:nb],
                                         op0=ALU.is_equal, op1=ALU.add).then_inc(nf_safe, 1)
                dve.wait_ge(nf_safe, q + 1)
                dve.reciprocal(rmax[:, 0:nb], safe[:, slot, 0:nb]).then_inc(nf_rmax, 1)

            def chain(q, cols, t):
                i = ORDER[t]
                n = BOUNDS * q + t
                dve.wait_ge(nf_signed, n + 1)
                if t < 2:
                    wait(dve, nf_summed, q)
                else:
                    dve.wait_ge(nf_chained, n - 1)
                up = i >= ZERO
                acc = nf_pos if up else nf_neg
                code = float(CODE[i + 1]) if up else -float(CODE[i])
                op = ALU.max if up else ALU.min
                mask_ = nf_sign[:, t % RING, 0:cols]
                if t < 2:
                    ins = dve.tensor_scalar(acc[:, 0:cols], mask_, code, 0.0, ALU.mult, op)
                else:
                    ins = dve.scalar_tensor_tensor(acc[:, 0:cols], mask_, code, acc[:, 0:cols], op0=ALU.mult, op1=op)
                ins.then_inc(nf_chained, 1)

            def layer_stats(n, b):
                dve.bn_stats(stats[:, b, :], resid[:, b, :]).then_inc(ln_stats, 1)
                dve.wait_ge(ln_stats, n + 1)
                dve.bn_aggr(mv[:, b, :], stats[:, b, :]).then_inc(ln_mv, 1)

            def layer_norm(n, b):
                dve.wait_ge(ln_rstd, n // 4 + 1)
                wait(dve, ln_turned, n - 1)
                if n == B:
                    dve.wait_ge(s_ready, N)
                dve.tensor_scalar(qT_sb[:, n % 2, :], resid[:, b, :], mv[:, b, 0:1], rstd[:, b:b + 1],
                                  ALU.subtract, ALU.mult).then_inc(ln_x, 1)

            def turn_x_lo(n, b):
                dve.wait_ge(ln_hi, n + 1)
                dve.tensor_tensor(xT_lo[:, :, b * S:(b + 1) * S], heads(x_ps(n)[:, :]),
                                  xT_hi[:, :, b * S:(b + 1) * S], ALU.subtract).then_inc(ln_lo, 1)

            for k in range(KT):
                dve.wait_ge(ctx_hi_done, k + 1)
                dve.tensor_tensor(ctx_lo[:, k, 0:512], ctx_raw[0][:, k, :], ctx_hi[:, k, 0:512], ALU.subtract)\
                    .then_inc(ctx_lo_done, 1)
            for k in range(KT):
                dve.wait_ge(ctx_hi_done, KT + k + 1)
                dve.tensor_tensor(ctx_lo[:, k, 512:1024], ctx_raw[1][:, k, :], ctx_hi[:, k, 512:1024], ALU.subtract)\
                    .then_inc(ctx_lo_done, 1)
            nf_prep(0, 0, cols_of(0))
            dve.wait_ge(small_in, 32)
            dve.tensor_tensor(wqk[:, :], qn_sb[:, :], kn_sb[:, :], ALU.mult).then_inc(wqk_done, 1)
            dve.wait_ge(wqk_done, 1)
            dve.tensor_scalar(wqk[:, :], wqk[:, :], float(np.sqrt(HD)), None, ALU.mult).then_inc(wqk_done, 1)

            def ssq_k(c):
                dve.wait_ge(kv_squared, c + 1)
                wait(dve, kv_rk, c - 3)
                dve.tensor_reduce(ssq[:, c % 4, :], heads(sq_sb[:, :]), AX.X, ALU.add).then_inc(kv_ssq, 1)

            def norm_k(c):
                dve.wait_ge(kv_rk, c + 1)
                wait(dve, k_turned, c - 1)
                dve.tensor_tensor(heads(q_sb[:, c % 2, :]), heads(kv_ps[c % 4][:, :]),
                                  rq[:, c % 4, :].unsqueeze(2).to_broadcast([P, J, HD]), ALU.mult).then_inc(k_normed, 1)

            dve.wait_ge(x_in, 16)
            for c in range(KV_UNITS):
                if c < KV_SLABS * B:
                    ssq_k(c)
                if 0 <= c - 1 < KV_SLABS * B:
                    norm_k(c - 1)
                if c < B:
                    layer_stats(c, c)
                if 0 <= c - 21 < B:
                    turn_x_lo(c - 21, c - 21)
                if 0 <= c - 18 < B:
                    layer_norm(c - 18, c - 18)
                lo, hi = spread(0, Q0 * BOUNDS, KV_UNITS)[c]
                for t in range(lo, hi):
                    chain(t // BOUNDS, cols_of(t // BOUNDS), t % BOUNDS)
                    if t % BOUNDS == 10:
                        q = t // BOUNDS + 1
                        nf_prep(q, q % 3, cols_of(q))

            def step(g, s):
                mine = not isinstance(g, int) or g < G

                def chains(part):
                    for c, t in bounds_in(g, s, part, 0):
                        chain(Q0 + 3 * g + c, QC, t)

                _, _, n = at(g, s, 1)
                if live(n):
                    dve.wait_ge(q_squared, n + 1)
                    wait(dve, q_rq, n - 3)
                    dve.tensor_reduce(ssq[:, (s - 1) % 4, :], heads(sq_sb[:, :]), AX.X, ALU.add).then_inc(q_ssq, 1)
                chains(0)

                _, _, n = at(g, s, 2)
                if live(n):
                    r = n_par(s, 2)
                    dve.wait_ge(p_exp, n + 1)
                    dve.reciprocal(rsum[:, r, :], psum_[:, r, :]).then_inc(p_rsum, 1)

                chains(1)
                _, b, n = at(g, s, 4)
                if live(n):
                    dve.wait_ge(attn_ready, n + 1)
                    wait(dve, attn_added, n)
                    dve.tensor_tensor(resid[:, b, :], resid[:, b, :], attn_ps[:, :], ALU.add).then_inc(attn_added, 1)
                if mine and s in WO_STEP:
                    for j in WO_STEP[s]:
                        dve.wait_ge(wo_in[j], 16 * (g + 1))
                        wait(dve, attn_ready, B * (g - 1) if s < 2 else B * g)
                        if isinstance(g, int) and g == 0:
                            dve.wait_ge(kv_ready, KV_UNITS)
                        dve.tensor_copy(wo_part(0, g, j), wo_raw[:, j, :]).then_inc(wo_hi_done, 1)
                if mine and s < KT and not (isinstance(g, int) and g == G - 1):
                    first = isinstance(g, int) and g == 0
                    dve.wait_ge(raw_in[s], 16 * (2 * KV_SLABS + 2 + g))
                    dve.wait_ge(kv_ready if first else q_ready, KV_UNITS if first else B * g)
                    dve.tensor_copy(ring[:, (g + 1) % 2, 0, s, :], raw[:, s, :]).then_inc(slab_hi, 1)

                _, _, n = at(g, s, 3)
                if live(n):
                    r = n_par(s, 3)
                    dve.wait_ge(oT_hi, n + 1)
                    dve.tensor_tensor(o_lo_sb[:, r, :], oT_ps[:, :], o_hi_sb[:, r, :], ALU.subtract).then_inc(oT_lo, 1)

                _, _, n = at(g, s, 1)
                if live(n):
                    r = n_par(s, 1)
                    dve.wait_ge(s_ready, n + 1)
                    dve.wait_ge(q_rq, n + 1)
                    wait(dve, p_exp, n - 1)
                    if isinstance(n, int) and n == 0:
                        dve.wait_ge(mask_in, 16)
                    for j in range(J):
                        ins = dve.scalar_tensor_tensor(s_sb[:, r, j * S:(j + 1) * S], s_ps[r][:, j * S:(j + 1) * S],
                                                       rq[:, (s - 1) % 4, j:j + 1], mask_sb[:, :],
                                                       op0=ALU.mult, op1=ALU.add)
                    ins.then_inc(s_scaled, 1)
                    dve.wait_ge(s_scaled, n + 1)
                    dve.tensor_reduce(nmax[:, r, :], heads(s_sb[:, r, :]), AX.X, ALU.max, negate=True).then_inc(s_max, 1)

                chains(2)
                if mine and s in (0, 3):
                    nf_prep(Q0 + 3 * g + 1 + s // 3, 1 + s // 3, QC)
                if mine and s == 5 and not (isinstance(g, int) and g == G - 1):
                    nf_prep(Q0 + 3 * g + 3, 0, QC)

            for s in range(B):
                step(0, s)
            with dve.Fori(1, G - 1) as g:
                for s in range(B):
                    step(g, s)
            for s in range(B):
                step(G - 1, s)
            def stats_of(b):
                dve.wait_ge(attn_added, N - B + b + 1)
                layer_stats(B + b, b)

            for s in range(4):
                if s == 0:
                    for b in range(4):
                        stats_of(b)
                step(G, s)
                if s == 1:
                    layer_norm(B, 0)
                    layer_norm(B + 1, 1)
                if s == 2:
                    turn_x_lo(B, 0)
                    layer_norm(B + 2, 2)
                    turn_x_lo(B + 1, 1)
                    layer_norm(B + 3, 3)
                if s == 3:
                    for b in range(4, B):
                        stats_of(b)
                    turn_x_lo(B + 2, 2)
                    layer_norm(B + 4, 4)
                    turn_x_lo(B + 3, 3)
                    layer_norm(B + 5, 5)

            def split_w(t, par, M, parts):
                for c in parts:
                    u = 3 * t + c
                    dve.wait_ge(w_hi, u + 1)
                    bank = wT_ps[(3 * par + c) % 2]
                    if c < 2:
                        dve.tensor_tensor(wT_part(par, c, 1, M), bank[:, 0:KT * M].rearrange("p (k m) -> p k m", k=KT),
                                          wT_part(par, c, 0, M), ALU.subtract).then_inc(w_lo, 1)
                    else:
                        dve.tensor_tensor(w3_part(par, 1, M), bank[0:M, :], w3_part(par, 0, M), ALU.subtract)\
                            .then_inc(w_lo, 1)

            def hidden(t, M, half):
                v = 2 * t + half
                dve.wait_ge(silu_done, v + 1)
                dve.wait_ge(up_ready, v + 1)
                wait(dve, h_lo, v - 1)
                dve.tensor_tensor(h_sb[0:M, half, :], s_ps[half][0:M, :], silu_sb[0:M, half, :], ALU.mult).then_inc(h_done, 1)

            def hidden_lo(t, par, M, half):
                dve.wait_ge(h_hi, 2 * t + half + 1)
                dve.tensor_tensor(hT_lo[0:M, par, half * 512:(half + 1) * 512], h_sb[0:M, half, :],
                                  hT_hi[0:M, par, half * 512:(half + 1) * 512], ALU.subtract).then_inc(h_lo, 1)

            def add_down(t, m):
                dve.wait_ge(down_ready, B * t + m + 1)
                wait(dve, down_added, B * t + m)
                dve.tensor_tensor(resid[:, m, :], resid[:, m, :], down_ps[m % 2][:, :], ALU.add).then_inc(down_added, 1)

            def ffn(t, par):
                if has_tile(t - 1):
                    split_w(t - 1, 1 - par, rows_of(t - 1), [2])
                for half in range(2):
                    if has_tile(t - 2):
                        for m in (4 * half, 4 * half + 1):
                            add_down(t - 2, m)
                    if has_tile(t):
                        split_w(t, par, rows_of(t), [half])
                    if isinstance(t, int) and t == 1 and half == 0:
                        for b in range(4, B):
                            turn_x_lo(B + b, b)
                            if b + 2 < B:
                                layer_norm(B + b + 2, b + 2)
                    if has_tile(t - 1):
                        hidden(t - 1, rows_of(t - 1), half)
                    if has_tile(t - 2):
                        for m in (4 * half + 2, 4 * half + 3):
                            add_down(t - 2, m)
                    if has_tile(t - 1):
                        hidden_lo(t - 1, 1 - par, rows_of(t - 1), half)

            for t in range(4):
                ffn(t, t % 2)
            with dve.Fori(2, FT // 2) as tt:
                for par in range(2):
                    ffn(tt * 2 + par, par)
            for t in range(FT, TILES + 2):
                ffn(t, t % 2)

        @block.gpsimd
        def _(pool):
            def low_part(dst, src, hi):
                return pool.tensor_tensor(dst, src, hi, ALU.subtract)

            def slab_part(m, k, dst):
                pool.wait_ge(slab_hi, KT * m + k + 1)
                low_part(dst[:, 1, k, :], raw[:, k, :], dst[:, 0, k, :]).then_inc(slab_lo, 1)

            def blocks(ap, cols):
                return ap.rearrange("p (b e) -> p b e", e=BLK)

            def nf_norm(q, slot, cols):
                nb = cols // BLK
                pool.wait_ge(nf_rmax, q + 1)
                wait(pool, nf_signed, BOUNDS * (q - 2))
                pool.tensor_tensor(blocks(nf_n[:, slot, 0:cols], cols), blocks(nf_raw[:, 0:cols], cols),
                                   rmax[:, 0:nb].unsqueeze(2).to_broadcast([P, nb, BLK]), ALU.mult).then_inc(nf_normed, 1)

            def nf_sum(q, cols):
                pool.wait_ge(nf_chained, BOUNDS * (q + 1))
                wait(pool, nf_out, 16 * q)
                pool.tensor_tensor(nf_dq[:, 0:cols], nf_pos[:, 0:cols], nf_neg[:, 0:cols], ALU.add).then_inc(nf_summed, 1)

            def nf_scale(q, slot, cols):
                nb = cols // BLK
                pool.wait_ge(nf_summed, q + 1)
                v = blocks(nf_dq[:, 0:cols], cols)
                pool.tensor_tensor(v, v, safe[:, slot, 0:nb].unsqueeze(2).to_broadcast([P, nb, BLK]), ALU.mult)\
                    .then_inc(nf_scaled, 1)

            pool.memset(ident[:, :], 0.0).then_inc(const_zero, 1)
            pool.memset(neg_half[:, :], -0.5).then_inc(const_set, 1)
            pool.memset(hd_eps[:, :], HD * EPS).then_inc(const_set, 1)
            pool.memset(ln_eps[:, :], LN_EPS).then_inc(const_set, 1)
            pool.wait_ge(const_zero, 1)
            pool.affine_select(out=ident[:, :], in_=ident[:, :], compare_op=ALU.not_equal, fill=1.0, base=0,
                               pattern=[[-1, P]], channel_multiplier=1).then_inc(const_done, 1)
            pool.wait_ge(const_set, 3)

            for k in range(KT):
                slab_part(0, k, slab_slot(0))
            nf_norm(0, 0, cols_of(0))
            for k in range(KT):
                slab_part(1, k, slab_slot(1))

            def rms(n, slot, ssq_sem, var_sem, out_sem):
                pool.wait_ge(ssq_sem, n + 1)
                wait(pool, out_sem, n)
                pool.tensor_tensor(var[:, :], ssq[:, slot, :], hd_eps[:, :], ALU.add).then_inc(var_sem, 1)
                pool.wait_ge(var_sem, n + 1)
                pool.tensor_tensor(rq[:, slot, :], var[:, :], neg_half[:, 0:J], ALU.pow).then_inc(out_sem, 1)

            def ln_scale(r):
                half = slice(4 * (r % 2), 4 * (r % 2) + 4)
                pool.wait_ge(ln_mv, 4 * (r + 1))
                pool.tensor_tensor(ln_var_sb[:, half], mv[:, half, 1], ln_eps[:, :], ALU.add).then_inc(ln_var, 1)
                pool.wait_ge(ln_var, r + 1)
                pool.tensor_tensor(rstd[:, half], ln_var_sb[:, half], neg_half[:, 0:4], ALU.pow).then_inc(ln_rstd, 1)

            for c in range(KV_UNITS):
                m, b, is_k = kv_kind(c)
                if is_k:
                    wait(pool, k_normed, c - 3)
                    rms(c, c % 4, kv_ssq, kv_var, kv_rk)
                if c == 12:
                    ln_scale(0)
                    ln_scale(1)
                if m >= 1 and m < 4 and b < KT:
                    slab_part(m + 1, b, slab_slot(m + 1))
                lo, hi = spread(0, Q0 * BOUNDS, KV_UNITS)[c]
                for t in range(lo, hi):
                    q = t // BOUNDS
                    if t % BOUNDS == 12:
                        nf_norm(q + 1, (q + 1) % 3, cols_of(q + 1))
                    if t % BOUNDS == BOUNDS - 1:
                        nf_sum(q, cols_of(q))
                        nf_scale(q, q % 3, cols_of(q))

            def step(g, s):
                q = Q0 + 3 * g
                mine = not isinstance(g, int) or g < G
                last = isinstance(g, int) and g == G - 1
                _, _, n = at(g, s, 1)
                if live(n):
                    wait(pool, s_scaled, n - 3)
                    rms(n, (s - 1) % 4, q_ssq, q_var, q_rq)
                _, _, n = at(g, s, 2)
                if live(n):
                    r = n_par(s, 2)
                    pool.wait_ge(p_rsum, n + 1)
                    v = heads(p_sb[:, r, :])
                    pool.tensor_tensor(v, v, rsum[:, r, :].unsqueeze(2).to_broadcast([P, J, S]), ALU.mult)\
                        .then_inc(p_normed, 1)
                if mine and s in WO_STEP:
                    for j in WO_STEP[s]:
                        pool.wait_ge(wo_hi_done, J * g + j + 1)
                        low_part(wo_part(1, g, j), wo_raw[:, j, :], wo_part(0, g, j)).then_inc(wo_lo_done, 1)
                if mine and s in (1, 4):
                    nf_norm(q + (s + 2) // 3, (s + 2) // 3, QC)
                if mine and s == 6 and not last:
                    nf_norm(q + 3, 0, QC)
                if mine and s in (3, 6):
                    nf_scale(q + s // 3 - 1, s // 3 - 1, QC)
                if s == 0 and not (isinstance(g, int) and g == 0):
                    nf_scale(q - 1, 2, QC)
                if mine and s < KT and not last:
                    slab_part(2 * KV_SLABS + 1 + g, s, ring[:, (g + 1) % 2, :, :, :])
                if mine and s in (2, 5, 7):
                    nf_sum(q + s // 3, QC)

            for s in range(B):
                step(0, s)
            with pool.Fori(1, G - 1) as g:
                for s in range(B):
                    step(g, s)
            for s in range(B):
                step(G - 1, s)
            for s in range(4):
                if s == 1:
                    ln_scale(2)
                step(G, s)
            ln_scale(3)


_OUT = ((B, S, D), "float32")


def kernel(**inputs):
    import numpy as _np
    import concourse.bacc as _bacc
    from concourse import mybir as _mybir
    from concourse.bass_utils import run_bass_kernel_spmd as _run

    a = {k: _np.asarray(v) for k, v in inputs.items()}
    laid = {
        "x": a["x"],
        "ctxT": a["ctx_4096"].reshape(B * S, D).T,
        "mask": a["mask_1x1xSxS2_ff0"],
        "wqT": a["L0_xattn_q_proj_w"].T,
        "wkT": a["L0_xattn_k_proj_w"].T,
        "wvT": a["L0_xattn_v_proj_w"].T,
        "woT": a["L0_xattn_o_proj_w"].T,
        "qnw": a["L0_xattn_q_norm_w"],
        "knw": a["L0_xattn_k_norm_w"],
        "w1": a["L0_ffn_w1"].reshape(P, FLAT),
        "w2": a["L0_ffn_w2"].reshape(P, FLAT),
        "w3": a["L0_ffn_w3"].reshape(P, FLAT),
    }
    nc = _bacc.Bacc("TRN2", target_bir_lowering=False, num_devices=1)
    arrays, args = {}, []
    for name, v in laid.items():
        v = _np.ascontiguousarray(v)
        arrays[f"in_{name}"] = v
        args.append(nc.dram_tensor(f"in_{name}", v.shape, _mybir.dt.from_np(v.dtype), kind="ExternalInput").ap())
    out = nc.dram_tensor("out_0", _OUT[0], _mybir.dt.from_np(_np.dtype(_OUT[1])), kind="ExternalOutput").ap()
    build(nc, *args, out)
    r = _run(nc, [arrays], core_ids=[0])
    return r.results[0]["out_0"]
```

```python
import concourse.bass as bass
from concourse import mybir
from contextlib import ExitStack
import numpy as np

F32 = mybir.dt.float32
F32R = mybir.dt.float32r
BF16 = mybir.dt.bfloat16
ALU = mybir.AluOpType
ACT = mybir.ActivationFunctionType
AX = mybir.AxisListType

P = 128
B = 8
S = 128
D = 512
KT = D // P
HD = 128
G = 8
J = 4
N = G * B
F = 1376
FT = F // P
FR = F - FT * P
TILES = FT + 1
EPS = 1e-5
LN_EPS = 1e-5
GC = D // HD
KV_SLABS = G // GC
KV_UNITS = 2 * KV_SLABS * B

CODE = np.array([-1.0, -0.6961928009986877, -0.5250730514526367, -0.39491748809814453,
                 -0.28444138169288635, -0.18477343022823334, -0.09105003625154495, 0.0,
                 0.07958029955625534, 0.16093020141124725, 0.24611230194568634, 0.33791524171829224,
                 0.44070982933044434, 0.5626170039176941, 0.7229568362236023, 1.0], np.float32)
BOUND = ((CODE[:-1] + CODE[1:]) * np.float32(0.5)).astype(np.float32)
ZERO = 7
BOUNDS = len(BOUND)
BLK = 64
FLAT = F * D // P
W3R = FLAT // F
COLS = FLAT + TILES * 2 * D
QC = 512
CHUNKS = -(-COLS // QC)
FIRST = COLS - (CHUNKS - 1) * QC
FQ = 6
FQ_STEP = 4
Q0 = CHUNKS - 3 * G - FQ
QF = CHUNKS - FQ
W3_CHUNKS = 1 + (FLAT - FIRST) // QC
assert FLAT % F == 0 and FIRST % BLK == 0 and (FLAT - FIRST) % QC == 0 and D == QC and Q0 % 3 == 0
ORDER = [7, 0, 8, 1, 9, 2, 10, 3, 11, 4, 12, 5, 13, 6, 14]
RING = 5


def build(nc, x, ctxT, mask, wqT, wkT, wvT, woT, qnw, knw, wff, out):
    dq_dram = nc.dram_tensor("dq_scratch", [P, COLS], F32).ap()
    v_dram = nc.dram_tensor("v_scratch", [G, P, B, HD], F32).ap()
    dq3 = dq_dram[:, 0:FLAT].rearrange("p (r h) -> p r h", r=W3R)
    wq_v = wqT.rearrange("(k p) n -> p k n", p=P)
    wk_v = wkT.rearrange("(k p) n -> p k n", p=P)
    wv_v = wvT.rearrange("(k p) n -> p k n", p=P)
    wo_v = woT.rearrange("(h p) n -> p h n", p=P)
    ctx_v = ctxT.rearrange("(k p) n -> p k n", p=P)

    es = ExitStack()
    with es:
        def sb(name, shape, dt=F32):
            return es.enter_context(nc.sbuf_tensor(name, shape, dt))

        def ps(name):
            return es.enter_context(nc.psum_tensor(name, [P, 512], F32))

        def sem(name):
            return es.enter_context(nc.semaphore(name))

        resid = sb("resid", [P, B, D])
        xT_hi = sb("xT_hi", [P, KT, B * S], F32R)
        xT_lo = sb("xT_lo", [P, KT, B * S], F32R)
        early = sb("early", [P, 2 * KT * B * S], F32R)
        ctx_hi = early[:, 0:KT * B * S].rearrange("p (k n) -> p k n", k=KT)
        ctx_lo = early[:, KT * B * S:].rearrange("p (k n) -> p k n", k=KT)
        wo_sb = early[:, 0:6144].rearrange("p (j l n) -> p j l n", j=6, l=2)
        o_hi_sb = early[:, 6144:7168].rearrange("p (r n) -> p r n", r=2)
        o_lo_sb = early[:, 7168:8192].rearrange("p (r n) -> p r n", r=2)
        hT_hi = early[:, 0:2048].rearrange("p (r n) -> p r n", r=2)
        hT_lo = early[:, 2048:4096].rearrange("p (r n) -> p r n", r=2)
        kT = sb("kT", [P, G, B * S])
        ring = sb("ring", [P, 2, 2, KT, 512], F32R)
        wT = ring[:, :, :, :, :].rearrange("p s l k n -> p s (l k n)")
        raw = sb("raw", [P, KT, 512])
        wo_raw = sb("wo_raw", [P, J, 512])
        v_sb = sb("v_sb", [P, B, HD])
        wqk = sb("wqk", [P, 1])
        qn_sb = sb("qn_sb", [P, 1])
        kn_sb = sb("kn_sb", [P, 1])
        mask_sb = sb("mask_sb", [P, S])
        ident = sb("ident", [P, P])
        neg_half = sb("neg_half", [P, B])
        hd_eps = sb("hd_eps", [P, J])
        ln_eps = sb("ln_eps", [P, 4])
        q_sb = sb("q_sb", [P, 2, 512])
        sq_sb = sb("sq_sb", [P, 512])
        qT_sb = sb("qT_sb", [P, 2, 512])
        sp_sb = sb("sp_sb", [P, 4, 512])
        s_sb = sp_sb[:, 0:2, :]
        p_sb = sp_sb[:, 2:4, :]
        pT_sb = sb("pT_sb", [P, 2, 512])
        ctx_raw = [wo_raw[:, :, :], sp_sb[:, :, :]]
        ssq = sb("ssq", [P, 4, J])
        var = sb("var", [P, J])
        ln_var_sb = sb("ln_var_sb", [P, B])
        rq = sb("rq", [P, 4, J])
        nmax = sb("nmax", [P, 2, J])
        psum_ = sb("psum_", [P, 2, J])
        rsum = sb("rsum", [P, 2, J])
        stats = sb("stats", [P, B, 6])
        mv = sb("mv", [P, B, 2])
        rstd = sb("rstd", [P, B])
        nf_raw = sb("nf_raw", [P, QC])
        nf_n = sb("nf_n", [P, 3, QC])
        nf_sign = sb("nf_sign", [P, RING, QC], BF16)
        nf_pos = sb("nf_pos", [P, QC])
        nf_neg = sb("nf_neg", [P, QC])
        nf_dq = sb("nf_dq", [P, QC])
        amax = sb("amax", [P, QC // BLK])
        safe = sb("safe", [P, 3, QC // BLK])
        rmax = sb("rmax", [P, QC // BLK])
        wn = kT[:, :, :].rearrange("p g n -> p (g n)")[:, 0:2 * 1536].rearrange("p (s c n) -> p s c n", s=2, c=3)
        side_sb = q_sb
        silu_sb = s_sb
        h_sb = p_sb

        proj_ps = [ps("proj_ps0"), ps("proj_ps1")]
        turn_ps = ps("turn_ps")
        s_ps = [ps("s_ps0"), ps("s_ps1")]
        pT_ps = ps("pT_ps")
        oT_ps = ps("oT_ps")
        attn_ps = ps("attn_ps")

        x_in, small_in, mask_in = sem("x_in"), sem("small_in"), sem("mask_in")
        ctx_in = [sem(f"ctx_in{b}") for b in range(B)]
        raw_in = [sem(f"raw_in{k}") for k in range(KT)]
        wo_in = [sem(f"wo_in{j}") for j in range(J)]
        v_in = [sem("v_in0"), sem("v_in1")]
        v_out = [sem("v_out0"), sem("v_out1")]
        nf_in, nf_out = sem("nf_in"), sem("nf_out")
        wn_in = [[sem(f"w{c + 1}_in{par}") for par in range(2)] for c in range(3)]
        y_out = sem("y_out")
        const_zero, const_set, const_done, wqk_done = (sem(n) for n in ("const_zero", "const_set", "const_done", "wqk_done"))
        ctx_hi_done, ctx_lo_done = sem("ctx_hi_done"), sem("ctx_lo_done")
        slab_hi, slab_lo = sem("slab_hi"), sem("slab_lo")
        wo_hi_done, wo_lo_done = sem("wo_hi_done"), sem("wo_lo_done")
        kv_ready, kv_squared, kv_ssq, kv_var, kv_rk = (sem(n) for n in ("kv_ready", "kv_squared", "kv_ssq", "kv_var", "kv_rk"))
        k_normed, k_turned, k_stored, v_copied = (sem(n) for n in ("k_normed", "k_turned", "k_stored", "v_copied"))
        ln_stats, ln_mv, ln_var, ln_rstd, ln_x, ln_turned, ln_hi, ln_lo = (
            sem(n) for n in ("ln_stats", "ln_mv", "ln_var", "ln_rstd", "ln_x", "ln_turned", "ln_hi", "ln_lo"))
        q_ready, q_copied, q_squared, q_ssq, q_var, q_rq = (
            sem(n) for n in ("q_ready", "q_copied", "q_squared", "q_ssq", "q_var", "q_rq"))
        qT_ready, qT_copied, s_ready, s_scaled, s_max, p_exp, p_rsum, p_normed = (
            sem(n) for n in ("qT_ready", "qT_copied", "s_ready", "s_scaled", "s_max", "p_exp", "p_rsum", "p_normed"))
        pT_ready, pT_copied, oT_ready, oT_hi, oT_lo, attn_ready, attn_added = (
            sem(n) for n in ("pT_ready", "pT_copied", "oT_ready", "oT_hi", "oT_lo", "attn_ready", "attn_added"))
        nf_amax, nf_safe, nf_rmax, nf_normed, nf_signed, nf_chained, nf_summed, nf_scaled = (
            sem(n) for n in ("nf_amax", "nf_safe", "nf_rmax", "nf_normed", "nf_signed", "nf_chained", "nf_summed", "nf_scaled"))
        w_turned, w_hi, w_lo, gate_ready, up_ready, silu_done, h_done, h_hi, h_lo, down_ready, down_added, side_copied, side_added = (
            sem(n) for n in ("w_turned", "w_hi", "w_lo", "gate_ready", "up_ready", "silu_done", "h_done",
                             "h_hi", "h_lo", "down_ready", "down_added", "side_copied", "side_added"))
        block = es.enter_context(nc.Block())

        def wait(eng, s, count):
            if not isinstance(count, int) or count > 0:
                eng.wait_ge(s, count)

        def live(n):
            return not isinstance(n, int) or 0 <= n < N

        def wo_part(l, g, j):
            return wo_sb[:, 2 + j, l, :] if j >= 2 else wo_sb[:, (g % 2) * 2 + j, l, :]

        def ctx_batch(b):
            return ctx_raw[b // 4][:, :, b % 4 * S:(b % 4 + 1) * S]

        def slab_slot(m):
            return ring[:, m % 2, :, :, :]

        def heads(ap):
            return ap.rearrange("p (j n) -> p j n", j=J)

        def kv_kind(c):
            return c // B, c % B, c < KV_SLABS * B

        kv_ps = [proj_ps[0], proj_ps[1], s_ps[0], s_ps[1]]
        wT_ps = [turn_ps, pT_ps]

        def x_ps(n):
            if n < B:
                return (oT_ps, attn_ps)[n % 2]
            return kv_ps[n - B] if n < B + 4 else (oT_ps, attn_ps, proj_ps[1], s_ps[1])[n % 4]

        def x_rows(n):
            return qT_sb[:, n % 2, :] if n < B or n % 4 < 2 else q_sb[:, n % 2, :]

        SIDE = (3, 7)
        ADDED = [m for m in range(B) if m not in SIDE]
        LAST_ADD = len(ADDED) * (TILES - 1)

        def down_bank(t, m):
            banks = [oT_ps, attn_ps, turn_ps, pT_ps]
            return banks[m % 4] if isinstance(t, int) and t == TILES - 1 else banks[m % 2]

        def n_par(s, lag):
            return (s - lag) % 2

        def has_tile(t):
            return not isinstance(t, int) or 0 <= t < TILES

        def has_side(t):
            return not isinstance(t, int) or 0 <= t < TILES - 1

        def rows_of(t):
            return FR if isinstance(t, int) and t == TILES - 1 else P

        def wT_part(par, c, l, M):
            at = 2048 * l + 512 * c
            return wT[:, par, at:at + KT * M].rearrange("p (k m) -> p k m", k=KT)

        def by_row(ap):
            return ap.rearrange("p (n r) -> p r n", r=W3R)

        def w3_part(par, l, M):
            at = 2048 * l + 1024
            return wT[0:M, par, at:at + D]

        def chunk_ap(tensor, q):
            if isinstance(q, int) and q == 0:
                return tensor[:, 0:FIRST]
            return tensor[:, bass.ds((q - 1) * QC + FIRST, QC)]

        def cols_of(q):
            return FIRST if isinstance(q, int) and q == 0 else QC

        def early_bounds(c, lead):
            if c < NF_UNIT:
                return []
            lo, hi = (lead + (Q0 * BOUNDS + AHEAD) * (c + i - NF_UNIT) // (KV_UNITS - NF_UNIT) for i in range(2))
            return [divmod(n, BOUNDS) for n in range(0 if c == NF_UNIT else lo, hi)]

        NF_UNIT = 4
        WO_STEP = {0: [0], 1: [1], 3: [2, 3]}
        CUTS = [0, 2, 4, 6, 8, 10, 12, 14, 15, 17, 19, 21, 22, 24, 26, 28, 29, 30, 33, 35, 37, 39, 41, 43, 45]
        LEAD = 3
        AHEAD = 12

        def bounds_in(g, s, part, lead):
            if isinstance(g, int) and g >= G:
                return []
            lo, hi = (CUTS[3 * s + part + i] + lead for i in range(2))
            if isinstance(g, int) and g == 0:
                lo = max(lo, AHEAD + lead)
            end = 3 * BOUNDS if isinstance(g, int) and g == G - 1 else hi
            return [divmod(n, BOUNDS) for n in range(lo, min(hi, end))]

        @block.sync
        def _(sp):
            def load_slab(m, src):
                for k in range(KT):
                    wait(sp, slab_lo, (m - 1) * KT + k + 1)
                    sp.dma_start(raw[:, k, :], src[:, k, :]).then_inc(raw_in[k], 16)

            def load_wo(g):
                for j in range(J):
                    wait(sp, wo_lo_done, (g - 1) * J + j + 1)
                    sp.dma_start(wo_raw[:, j, :], wo_v[:, g * J + j, :]).then_inc(wo_in[j], 16)

            def load_v(g, half):
                wait(sp, oT_ready, g * B - (4 if half == 0 else 0))
                sp.dma_start(v_sb[:, 4 * half:4 * half + 4, :], v_dram[g, :, 4 * half:4 * half + 4, :])\
                    .then_inc(v_in[half], 16)

            def nf_load(q):
                wait(sp, nf_normed, q)
                sp.dma_start(nf_raw[:, 0:cols_of(q)], chunk_ap(wff, q)).then_inc(nf_in, 16)

            def nf_store(q):
                wait(sp, nf_scaled, q + 1)
                sp.dma_start(chunk_ap(dq_dram, q), nf_dq[:, 0:cols_of(q)]).then_inc(nf_out, 16)

            kv_src = [wk_v[:, :, 0:512], wk_v[:, :, 512:1024], wv_v[:, :, 0:512], wv_v[:, :, 512:1024]]

            def load_ctx(b):
                sp.dma_start(ctx_batch(b), ctx_v[:, :, b * S:(b + 1) * S]).then_inc(ctx_in[b], 16)

            load_ctx(0)
            load_slab(0, kv_src[0])
            for b in range(1, 4):
                load_ctx(b)
            sp.dma_start(qn_sb[:, :], qnw.rearrange("(p a) -> p a", a=1)).then_inc(small_in, 16)
            sp.dma_start(kn_sb[:, :], knw.rearrange("(p a) -> p a", a=1)).then_inc(small_in, 16)
            for b in range(4, B):
                load_ctx(b)
            nf_load(0)
            load_slab(1, kv_src[1])
            sp.dma_start(resid[:, :, :], x.rearrange("b s d -> s b d")).then_inc(x_in, 16)
            sp.dma_start(mask_sb[:, :], mask[0, 0, :, :]).then_inc(mask_in, 16)
            nf_load(1)
            load_slab(2, kv_src[2])
            load_slab(3, kv_src[3])
            nf_load(2)
            nf_store(0)
            load_slab(4, wq_v[:, :, 0:512])
            nf_load(3)
            nf_store(1)
            sp.wait_ge(ctx_lo_done, B)

            def body(g, last):
                q = Q0 + 3 * g
                nf_load(q + 1)
                load_wo(g)
                if not last:
                    load_slab(5 + g, wq_v[:, :, bass.ds((g + 1) * 512, 512)])
                if isinstance(g, int) and g == 0:
                    for p in range(2):
                        sp.wait_ge(v_out[p], 16 * KV_SLABS * B // 2)
                load_v(g, 0)
                nf_store(q - 1)
                load_v(g, 1)
                nf_load(q + 2)
                nf_store(q)
                if not last:
                    nf_load(q + 3)
                nf_store(q + 1)

            body(0, False)
            with sp.Fori(1, G - 1) as g:
                body(g, False)
            body(G - 1, True)

            sp.wait_ge(s_ready, N)

            def load_part(t, par, M, c):
                wait(sp, w_turned, 3 * (t - 2) + c + 1)
                if c < 2:
                    sp.wait_ge(nf_out, 16 * (W3_CHUNKS + 2 * t + c + 1))
                    sp.dma_start(wn[0:M, par, c, :], dq_dram[0:M, bass.ds(t * (2 * D) + (FLAT + c * D), D)])\
                        .then_inc(wn_in[c][par], 16)
                else:
                    sp.wait_ge(nf_out, 16 * W3_CHUNKS)
                    sp.dma_start(wn[:, par, 2, 0:KT * M].rearrange("p (r m) -> p r m", r=W3R),
                                 dq3[:, :, bass.ds(t * P, M)]).then_inc(wn_in[c][par], 16)

            def ffn(t, par, quantise):
                if quantise:
                    nf_load(t + (QF - FQ_STEP))
                    nf_store(t + (QF - FQ_STEP - 1))
                if has_tile(t):
                    load_part(t, par, rows_of(t), 1)
                if has_tile(t + 1):
                    load_part(t + 1, 1 - par, rows_of(t + 1), 0)
                    load_part(t + 1, 1 - par, rows_of(t + 1), 2)

            load_part(0, 0, P, 0)
            load_part(0, 0, P, 2)
            for t in range(FQ_STEP):
                ffn(t, t % 2, False)
            with sp.Fori(FQ_STEP // 2, (FQ_STEP + FQ) // 2 - 1) as tt:
                for par in range(2):
                    ffn(tt * 2 + par, par, True)
            for t in range(FQ_STEP + FQ - 2, FQ_STEP + FQ):
                ffn(t, t % 2, True)
            nf_store(CHUNKS - 1)
            load_part(TILES - 1, (TILES - 1) % 2, FR, 1)
            for m in range(B):
                sp.wait_ge(down_added, LAST_ADD + m + 1)
                sp.dma_start(out[m, :, :], resid[:, m, :]).then_inc(y_out, 16)
            sp.wait_ge(y_out, 16 * B)

        def in_phase0(g, s, lag):
            return isinstance(g, int) and g == 0 and s - lag in (0, 1)

        def at(g, s, lag):
            return g + (s - lag) // B, (s - lag) % B, B * g + s - lag

        @block.tensor
        def _(pe):
            def turn(bank, src, cols, rows=P):
                for k in range(len(src)):
                    mm = pe.transpose(bank[0:cols, k * rows:(k + 1) * rows], src[k], ident[0:rows, 0:rows])
                return mm

            def three_pass(bank, pairs):
                for n, (a_hi, a_lo, b_hi, b_lo) in enumerate(pairs):
                    pe.matmul(bank, a_hi, b_hi, start=(n == 0), stop=False)
                    pe.matmul(bank, a_hi, b_lo, start=False, stop=False)
                    mm = pe.matmul(bank, a_lo, b_hi, start=False, stop=(n == len(pairs) - 1))
                return mm

            def tokens(ap, k, b):
                return ap[:, k, b * S:(b + 1) * S]

            def kv(c):
                m, b, _ = kv_kind(c)
                if m == 0:
                    pe.wait_ge(ctx_lo_done, b + 1)
                if c > 0:
                    pe.wait_ge(slab_lo, KT * (m + 1))
                if 4 <= c < KV_SLABS * B + 4:
                    pe.wait_ge(k_normed, c - 3)
                elif c >= 4:
                    pe.wait_ge(v_copied, c - 3 - KV_SLABS * B)
                pairs = [(tokens(ctx_hi, k, b), tokens(ctx_lo, k, b), slab_slot(m)[:, 0, k, :], slab_slot(m)[:, 1, k, :])
                         for k in range(KT)]
                if c > 0:
                    three_pass(kv_ps[c % 4][:, :], pairs).then_inc(kv_ready, 1)
                    return
                for k, (a_hi, a_lo, b_hi, b_lo) in enumerate(pairs):
                    pe.wait_ge(slab_lo, k + 1)
                    pe.matmul(kv_ps[0][:, :], a_hi, b_hi, start=(k == 0), stop=False)
                    pe.matmul(kv_ps[0][:, :], a_hi, b_lo, start=False, stop=False)
                    mm = pe.matmul(kv_ps[0][:, :], a_lo, b_hi, start=False, stop=(k == KT - 1))
                mm.then_inc(kv_ready, 1)

            def turn_k(c):
                pe.wait_ge(k_normed, c + 1)
                wait(pe, k_stored, c)
                turn(turn_ps, [q_sb[:, c % 2, j * HD:(j + 1) * HD] for j in range(J)], P).then_inc(k_turned, 1)

            def turn_x(n):
                pe.wait_ge(ln_x, n + 1)
                if B <= n < B + 2:
                    pe.wait_ge(q_squared, N)
                elif B + 2 <= n < B + 4:
                    pe.wait_ge(s_scaled, N)
                elif n == B + 4:
                    pe.wait_ge(oT_lo, N)
                elif n == B + 5:
                    pe.wait_ge(attn_added, N)
                elif n >= B + 6:
                    pe.wait_ge(ln_lo, B + 4)
                if n < B:
                    wait(pe, ln_lo, n - 1)
                turn(x_ps(n), [x_rows(n)[:, k * P:(k + 1) * P] for k in range(KT)], P).then_inc(ln_turned, 1)

            def queries(g, s):
                gg, b, n = at(g, s, 0)
                if live(n):
                    pe.wait_ge(slab_lo, KT * (2 * KV_SLABS + gg + 1))
                    wait(pe, q_squared, n - 1)
                    if isinstance(n, int) and n < 2:
                        pe.wait_ge(v_copied, KV_SLABS * B - 3 + n)
                    if isinstance(n, int) and n < B:
                        pe.wait_ge(ln_lo, n + 1)
                    slab = ring[:, gg % 2, :, :, :]
                    three_pass(proj_ps[n_par(s, 0)][:, :], [
                        (tokens(xT_hi, k, b), tokens(xT_lo, k, b), slab[:, 0, k, :], slab[:, 1, k, :])
                        for k in range(KT)]).then_inc(q_ready, 1)

            pe.wait_ge(const_done, 1)
            for c in range(KV_UNITS):
                if c >= KV_UNITS - 2:
                    queries(0, c - KV_UNITS + 2)
                kv(c)
                if 0 <= c - 3 < KV_SLABS * B:
                    turn_k(c - 3)
                if 0 <= c - 17 < B:
                    turn_x(c - 17)

            def step(g, s):
                _, _, n = at(g, s, 3)
                if live(n):
                    pe.wait_ge(p_normed, n + 1)
                    wait(pe, pT_copied, n)
                    turn(pT_ps, [p_sb[:, n_par(s, 3), j * S:(j + 1) * S] for j in range(J)], P).then_inc(pT_ready, 1)

                def project(heads_of):
                    gg, _, n = at(g, s, 4)
                    if not live(n):
                        return
                    if heads_of[0] == 0:
                        pe.wait_ge(oT_lo, n + 1)
                        wait(pe, attn_added, n)
                        if isinstance(n, int) and n == 0:
                            pe.wait_ge(ln_lo, B)
                    for j in heads_of:
                        pe.wait_ge(wo_lo_done, gg * J + j + 1)
                        r = n_par(s, 4)
                        oh, ol = (t[:, r, j * S:(j + 1) * S] for t in (o_hi_sb, o_lo_sb))
                        w_hi_, w_lo_ = (wo_part(l, gg, j) for l in range(2))
                        pe.matmul(attn_ps[:, :], oh, w_hi_, start=(j == 0), stop=False)
                        pe.matmul(attn_ps[:, :], oh, w_lo_, start=False, stop=False)
                        mm = pe.matmul(attn_ps[:, :], ol, w_hi_, start=False, stop=(j == J - 1))
                    if heads_of[-1] == J - 1:
                        mm.then_inc(attn_ready, 1)

                project([0, 1])

                _, _, n = at(g, s, 1)
                if live(n):
                    pe.wait_ge(q_copied, n + 1)
                    wait(pe, qT_copied, n)
                    if isinstance(n, int) and n == 0:
                        pe.wait_ge(k_stored, KV_SLABS * B)
                    turn(turn_ps, [q_sb[:, n_par(s, 1), j * HD:(j + 1) * HD] for j in range(J)], P).then_inc(qT_ready, 1)

                project([2, 3])

                gg, b, n = at(g, s, 3)
                if live(n):
                    pe.wait_ge(pT_copied, n + 1)
                    pe.wait_ge(v_in[b // 4], 16 * (gg + 1))
                    wait(pe, oT_lo, n)
                    if isinstance(n, int) and n == 0:
                        pe.wait_ge(ln_lo, B)
                    pe.matmul(oT_ps[:, :], v_sb[:, b, :], pT_sb[:, n_par(s, 3), :], start=True, stop=True)\
                        .then_inc(oT_ready, 1)

                gg, b, n = at(g, s, 1)
                if live(n):
                    pe.wait_ge(qT_copied, n + 1)
                    wait(pe, s_scaled, n - 1)
                    if isinstance(n, int) and n == 0:
                        pe.wait_ge(k_stored, KV_SLABS * B)
                        pe.wait_ge(v_copied, KV_SLABS * B)
                    for j in range(J):
                        mm = pe.matmul(s_ps[n_par(s, 1)][:, j * S:(j + 1) * S],
                                       qT_sb[:, n_par(s, 1), j * S:(j + 1) * S],
                                       kT[:, gg, b * S:(b + 1) * S], start=True, stop=True)
                    mm.then_inc(s_ready, 1)

                if not in_phase0(g, s, 0):
                    queries(g, s)

            for s in range(B):
                step(0, s)
            with pe.Fori(1, G) as g:
                for s in range(B):
                    step(g, s)

            def turn_w(t, par, M, parts):
                for c in parts:
                    pe.wait_ge(wn_in[c][par], 16 * (t // 2 + 1))
                    u = 3 * t + c
                    wait(pe, w_lo, u - 1)
                    if isinstance(t, int) and t == 0 and c == 0:
                        pe.wait_ge(qT_copied, N)
                    if isinstance(t, int) and t == 0 and c == 1:
                        pe.wait_ge(pT_copied, N)
                    bank = wT_ps[(3 * par + c) % 2]
                    if c < 2:
                        mm = turn(bank, [wn[0:M, par, c, k * P:(k + 1) * P] for k in range(KT)], P, M)
                    else:
                        mm = turn(bank, [wn[:, par, 2, r * M:(r + 1) * M] for r in range(KT)], M, P)
                    mm.then_inc(w_turned, 1)

            def product(bank, t, par, M, c, half, ready):
                pe.wait_ge(w_lo, 3 * t + c + 1)
                if isinstance(t, int) and t == 0:
                    pe.wait_ge(ln_lo, B + 4 * (half + 1))
                three_pass(bank[0:M, :], [
                    (wT_part(par, c, 0, M)[:, k, :], wT_part(par, c, 1, M)[:, k, :],
                     xT_hi[:, k, half * 512:(half + 1) * 512], xT_lo[:, k, half * 512:(half + 1) * 512])
                    for k in range(KT)]).then_inc(ready, 1)

            def gate(t, par, M, half):
                wait(pe, silu_done, 2 * t + half - 1)
                product(proj_ps[half], t, par, M, 0, half, gate_ready)

            def up(t, par, M, half):
                wait(pe, h_done, 2 * t + half - 1)
                product(s_ps[half], t, par, M, 1, half, up_ready)

            def down(t, par, M, m):
                pe.wait_ge(h_lo, 2 * t + m // 4 + 1)
                pe.wait_ge(w_lo, 3 * t + 3)
                if m == 1:
                    wait(pe, side_copied, 2 * t)
                elif isinstance(t, int) and t == TILES - 1 and m > 0:
                    wait(pe, down_added, LAST_ADD + m - 3)
                elif m >= 2 and m - 2 in SIDE:
                    wait(pe, side_copied, 2 * t + SIDE.index(m - 2) + 1)
                elif m >= 2:
                    wait(pe, down_added, len(ADDED) * t + ADDED.index(m - 2) + 1)
                else:
                    wait(pe, down_added, len(ADDED) * t)
                if isinstance(t, int) and t == 0 and m < 2:
                    pe.wait_ge(ln_lo, 2 * B)
                hh, hl = (a[0:M, par, m * S:(m + 1) * S] for a in (hT_hi, hT_lo))
                three_pass(down_bank(t, m)[:, :], [(hh, hl, w3_part(par, 0, M), w3_part(par, 1, M))])\
                    .then_inc(down_ready, 1)

            def ffn(t, par):
                if has_tile(t - 1):
                    turn_w(t - 1, 1 - par, rows_of(t - 1), [2])
                for half in range(2):
                    if has_tile(t - 1):
                        gate(t - 1, 1 - par, rows_of(t - 1), half)
                    if has_tile(t - 2):
                        for m in (4 * half, 4 * half + 1):
                            down(t - 2, par, rows_of(t - 2), m)
                    if has_tile(t):
                        turn_w(t, par, rows_of(t), [half])
                    if isinstance(t, int) and t == 1 and half == 0:
                        for n in range(B + 4, 2 * B):
                            turn_x(n)
                    if has_tile(t - 1):
                        up(t - 1, 1 - par, rows_of(t - 1), half)
                    if has_tile(t - 2):
                        for m in (4 * half + 2, 4 * half + 3):
                            down(t - 2, par, rows_of(t - 2), m)

            for s in range(4):
                if s == 3:
                    turn_w(0, 0, P, [0, 1])
                step(G, s)
                if s == 1:
                    for b in range(4):
                        turn_x(B + b)
            for t in range(1, 4):
                ffn(t, t % 2)
            with pe.Fori(2, FT // 2) as tt:
                for par in range(2):
                    ffn(tt * 2 + par, par)
            for t in range(FT, TILES + 2):
                ffn(t, t % 2)

        @block.scalar
        def _(act):
            def sign(q, slot, cols, t):
                i = ORDER[t]
                edge = BOUND[i] if i >= ZERO else np.nextafter(BOUND[i], np.float32(1))
                act.wait_ge(nf_normed, q + 1)
                wait(act, nf_chained, BOUNDS * q + t - RING + 1)
                act.activation(nf_sign[:, t % RING, 0:cols], nf_n[:, slot, 0:cols], ACT.Sign, bias=-float(edge))\
                    .then_inc(nf_signed, 1)

            def slab_part(m, k, dst, free, count):
                act.wait_ge(raw_in[k], 16 * (m + 1))
                wait(act, free, count)
                act.activation(dst[:, 0, k, :], raw[:, k, :], ACT.Copy).then_inc(slab_hi, 1)

            def turn_x_hi(n, b):
                act.wait_ge(ln_turned, n + 1)
                act.activation(xT_hi[:, :, b * S:(b + 1) * S], heads(x_ps(n)[:, :]), ACT.Copy).then_inc(ln_hi, 1)

            def ctx_high(b):
                act.wait_ge(ctx_in[b], 16)
                act.activation(ctx_hi[:, :, b * S:(b + 1) * S], ctx_batch(b), ACT.Copy).then_inc(ctx_hi_done, 1)

            ctx_high(0)
            for k in range(KT):
                slab_part(0, k, slab_slot(0), kv_ready, 0)
            ctx_high(1)

            def store_k(c):
                m, b, _ = kv_kind(c)
                act.wait_ge(k_turned, c + 1)
                act.wait_ge(wqk_done, 2)
                act.activation(kT[:, m * GC:(m + 1) * GC, b * S:(b + 1) * S], heads(turn_ps[:, :]), ACT.Copy,
                               scale=wqk[:, 0:1]).then_inc(k_stored, 1)

            def copy_turned(g, s):
                _, _, n = at(g, s, 1)
                if live(n):
                    act.wait_ge(qT_ready, n + 1)
                    wait(act, s_ready, n - 1)
                    act.activation(qT_sb[:, n_par(s, 1), :], turn_ps[:, :], ACT.Copy).then_inc(qT_copied, 1)

            def copy_queries(g, s):
                _, _, n = at(g, s, 1)
                if live(n):
                    r = n_par(s, 1)
                    act.wait_ge(q_ready, n + 1)
                    wait(act, qT_ready, n - 1)
                    if isinstance(n, int) and n == 0:
                        act.wait_ge(k_turned, KV_SLABS * B)
                    act.activation(q_sb[:, r, :], proj_ps[r][:, :], ACT.Copy).then_inc(q_copied, 1)
                    wait(act, q_ssq, n)
                    act.activation(sq_sb[:, :], proj_ps[r][:, :], ACT.Square).then_inc(q_squared, 1)

            for c in range(KV_UNITS):
                m, b, is_k = kv_kind(c)
                if 1 <= m < 4 and b < KT:
                    slab_part(m + 1, b, slab_slot(m + 1), kv_ready, B * m)
                if is_k:
                    act.wait_ge(kv_ready, c + 1)
                    wait(act, kv_ssq, c)
                    act.activation(sq_sb[:, :], kv_ps[c % 4][:, :], ACT.Square).then_inc(kv_squared, 1)
                else:
                    v = c - KV_SLABS * B
                    if c >= KV_UNITS - 2:
                        copy_queries(0, c - KV_UNITS + 3)
                    act.wait_ge(kv_ready, c + 1)
                    wait(act, v_out[v % 2], 16 * (v // 2))
                    act.activation(pT_sb[:, c % 2, :], kv_ps[c % 4][:, :], ACT.Copy).then_inc(v_copied, 1)
                    act.wait_ge(v_copied, v + 1)
                    h0 = (m - KV_SLABS) * GC
                    act.dma_start(v_dram[h0:h0 + GC, :, b, :].rearrange("g p d -> p g d"), heads(pT_sb[:, c % 2, :]))\
                        .then_inc(v_out[v % 2], 16)
                if c < B - 2:
                    ctx_high(c + 2)
                if 0 <= c - 2 < KT:
                    slab_part(1, c - 2, slab_slot(1), kv_ready, 0)
                if 0 <= c - 3 < KV_SLABS * B:
                    store_k(c - 3)
                if 0 <= c - 18 < B:
                    turn_x_hi(c - 18, c - 18)
                if c == KV_UNITS - 1:
                    copy_turned(0, 1)
                for q, t in early_bounds(c, LEAD):
                    sign(q, q % 3, cols_of(q), t)

            def step(g, s):
                def signs(part):
                    for c, t in bounds_in(g, s, part, LEAD):
                        sign(Q0 + 3 * g + c, c % 3, QC, t)

                filling = isinstance(g, int) and g == 0 and s <= 3
                if not in_phase0(g, s, 1):
                    copy_queries(g, s)

                _, _, n = at(g, s, 3)
                if live(n):
                    act.wait_ge(pT_ready, n + 1)
                    wait(act, oT_ready, n - 1)
                    if isinstance(n, int) and n < 2:
                        act.wait_ge(v_out[n], 16 * KV_SLABS * B // 2)
                    act.activation(pT_sb[:, n_par(s, 3), :], pT_ps[:, :], ACT.Copy).then_inc(pT_copied, 1)

                if filling and s >= 2:
                    copy_turned(g, s)

                _, _, n = at(g, s, 2)
                if live(n):
                    r = n_par(s, 2)
                    act.wait_ge(s_max, n + 1)
                    wait(act, pT_ready, n - 1)
                    for j in range(J):
                        e = act.activation(p_sb[:, r, j * S:(j + 1) * S], s_sb[:, r, j * S:(j + 1) * S], ACT.Exp,
                                           bias=nmax[:, r, j:j + 1], accum_out=psum_[:, r, j:j + 1])
                    e.then_inc(p_exp, 1)

                if not filling:
                    copy_turned(g, s)

                signs(0)

                _, _, n = at(g, s, 3)
                if live(n):
                    act.wait_ge(oT_ready, n + 1)
                    wait(act, attn_ready, n - 1)
                    if isinstance(n, int) and n == 0:
                        act.wait_ge(kv_ready, KV_UNITS)
                    act.activation(o_hi_sb[:, n_par(s, 3), :], oT_ps[:, :], ACT.Copy).then_inc(oT_hi, 1)

                signs(1)
                signs(2)

            for s in range(B):
                step(0, s)
            with act.Fori(1, G - 1) as g:
                for s in range(B):
                    step(g, s)
            for s in range(B):
                step(G - 1, s)


            def split_w(t, par, M, parts):
                for c in parts:
                    u = 3 * t + c
                    act.wait_ge(w_turned, u + 1)
                    bank = wT_ps[(3 * par + c) % 2]
                    if c < 2:
                        wait(act, up_ready, 2 * (t - 1))
                        act.activation(wT_part(par, c, 0, M), bank[:, 0:KT * M].rearrange("p (k m) -> p k m", k=KT),
                                       ACT.Copy).then_inc(w_hi, 1)
                    else:
                        wait(act, down_ready, B * (t - 1))
                        act.activation(by_row(w3_part(par, 0, M)), heads(bank[0:M, :]), ACT.Copy).then_inc(w_hi, 1)

            def silu(t, M, half):
                v = 2 * t + half
                act.wait_ge(gate_ready, v + 1)
                wait(act, h_done, v - 1)
                act.activation(silu_sb[0:M, half, :], proj_ps[half][0:M, :], ACT.Silu).then_inc(silu_done, 1)

            def hidden_hi(t, par, M, half):
                v = 2 * t + half
                act.wait_ge(h_done, v + 1)
                wait(act, down_ready, B * (t - 1))
                act.activation(hT_hi[0:M, par, half * 512:(half + 1) * 512], h_sb[0:M, half, :], ACT.Copy)\
                    .then_inc(h_hi, 1)

            def copy_side(t, half):
                n = 2 * t + half
                act.wait_ge(down_ready, B * t + SIDE[half] + 1)
                wait(act, side_added, n - 1)
                act.activation(side_sb[:, half, :], down_bank(t, SIDE[half])[:, :], ACT.Copy).then_inc(side_copied, 1)

            def ffn(t, par, quantise):
                def signs(lo, hi):
                    if quantise:
                        for n in range(lo, hi):
                            sign(t + (QF - FQ_STEP), 1 + par, QC, n)

                if has_tile(t - 1):
                    split_w(t - 1, 1 - par, rows_of(t - 1), [2])
                signs(0, 4)
                if has_tile(t - 1):
                    silu(t - 1, rows_of(t - 1), 0)
                if has_tile(t):
                    split_w(t, par, rows_of(t), [0])
                if isinstance(t, int) and t == 1:
                    for b in range(4, B):
                        turn_x_hi(B + b, b)
                signs(4, 10)
                if has_tile(t - 1):
                    hidden_hi(t - 1, 1 - par, rows_of(t - 1), 0)
                if has_side(t - 2):
                    copy_side(t - 2, 0)
                signs(10, 13)
                if has_tile(t - 1):
                    silu(t - 1, rows_of(t - 1), 1)
                if has_tile(t):
                    split_w(t, par, rows_of(t), [1])
                signs(13, 15)
                if has_tile(t - 1):
                    hidden_hi(t - 1, 1 - par, rows_of(t - 1), 1)
                if has_side(t - 2):
                    copy_side(t - 2, 1)

            for s in range(4):
                if s == 3:
                    split_w(0, 0, P, [0, 1])
                step(G, s)
                if s == 1:
                    for b in range(4):
                        turn_x_hi(B + b, b)
            for t in range(1, FQ_STEP):
                ffn(t, t % 2, False)
            with act.Fori(FQ_STEP // 2, (FQ_STEP + FQ) // 2) as tt:
                for par in range(2):
                    ffn(tt * 2 + par, par, True)
            for t in range(FQ_STEP + FQ, TILES + 2):
                ffn(t, t % 2, False)

        @block.vector
        def _(dve):
            def nf_prep(q, slot, cols, slots=3):
                nb = cols // BLK
                dve.wait_ge(nf_in, 16 * (q + 1))
                wait(dve, nf_scaled, q - slots + 1)
                dve.tensor_reduce(amax[:, 0:nb], nf_raw[:, 0:cols].rearrange("p (b e) -> p b e", e=BLK),
                                  AX.X, ALU.max, apply_absolute_value=True).then_inc(nf_amax, 1)
                dve.wait_ge(nf_amax, q + 1)
                dve.scalar_tensor_tensor(safe[:, slot, 0:nb], amax[:, 0:nb], 0.0, amax[:, 0:nb],
                                         op0=ALU.is_equal, op1=ALU.add).then_inc(nf_safe, 1)
                dve.wait_ge(nf_safe, q + 1)
                dve.reciprocal(rmax[:, 0:nb], safe[:, slot, 0:nb]).then_inc(nf_rmax, 1)

            def chain(q, cols, t):
                i = ORDER[t]
                n = BOUNDS * q + t
                dve.wait_ge(nf_signed, n + 1)
                if t < 2:
                    wait(dve, nf_summed, q)
                else:
                    dve.wait_ge(nf_chained, n - 1)
                up = i >= ZERO
                acc = nf_pos if up else nf_neg
                code = float(CODE[i + 1]) if up else -float(CODE[i])
                op = ALU.max if up else ALU.min
                mask_ = nf_sign[:, t % RING, 0:cols]
                if t < 2:
                    ins = dve.tensor_scalar(acc[:, 0:cols], mask_, code, 0.0, ALU.mult, op)
                else:
                    ins = dve.scalar_tensor_tensor(acc[:, 0:cols], mask_, code, acc[:, 0:cols], op0=ALU.mult, op1=op)
                ins.then_inc(nf_chained, 1)

            def layer_stats(n, b):
                dve.bn_stats(stats[:, b, :], resid[:, b, :]).then_inc(ln_stats, 1)
                dve.wait_ge(ln_stats, n + 1)
                dve.bn_aggr(mv[:, b, :], stats[:, b, :]).then_inc(ln_mv, 1)

            def layer_norm(n, b):
                dve.wait_ge(ln_rstd, n // 4 + 1)
                if n < B:
                    wait(dve, ln_turned, n - 1)
                elif n < B + 2:
                    dve.wait_ge(s_ready, N)
                elif n < B + 4:
                    dve.wait_ge(qT_ready, N)
                else:
                    dve.wait_ge(ln_turned, n - 3)
                dve.tensor_scalar(x_rows(n), resid[:, b, :], mv[:, b, 0:1], rstd[:, b:b + 1],
                                  ALU.subtract, ALU.mult).then_inc(ln_x, 1)

            def turn_x_lo(n, b):
                dve.wait_ge(ln_hi, n + 1)
                dve.tensor_tensor(xT_lo[:, :, b * S:(b + 1) * S], heads(x_ps(n)[:, :]),
                                  xT_hi[:, :, b * S:(b + 1) * S], ALU.subtract).then_inc(ln_lo, 1)

            def ctx_low(b):
                dve.wait_ge(ctx_hi_done, b + 1)
                at = slice(b * S, (b + 1) * S)
                dve.tensor_tensor(ctx_lo[:, :, at], ctx_batch(b), ctx_hi[:, :, at], ALU.subtract).then_inc(ctx_lo_done, 1)

            ctx_low(0)
            for k in range(KT):
                dve.wait_ge(slab_hi, k + 1)
                dve.tensor_tensor(slab_slot(0)[:, 1, k, :], raw[:, k, :], slab_slot(0)[:, 0, k, :], ALU.subtract)\
                    .then_inc(slab_lo, 1)
            ctx_low(1)
            def ssq_k(c):
                dve.wait_ge(kv_squared, c + 1)
                wait(dve, kv_rk, c - 3)
                dve.tensor_reduce(ssq[:, c % 4, :], heads(sq_sb[:, :]), AX.X, ALU.add).then_inc(kv_ssq, 1)

            def norm_k(c):
                dve.wait_ge(kv_rk, c + 1)
                wait(dve, k_turned, c - 1)
                dve.tensor_tensor(heads(q_sb[:, c % 2, :]), heads(kv_ps[c % 4][:, :]),
                                  rq[:, c % 4, :].unsqueeze(2).to_broadcast([P, J, HD]), ALU.mult).then_inc(k_normed, 1)

            def sum_squares(g, s):
                _, _, n = at(g, s, 1)
                if live(n):
                    dve.wait_ge(q_squared, n + 1)
                    wait(dve, q_rq, n - 3)
                    dve.tensor_reduce(ssq[:, (s - 1) % 4, :], heads(sq_sb[:, :]), AX.X, ALU.add).then_inc(q_ssq, 1)

            for c in range(KV_UNITS):
                if c < KV_SLABS * B:
                    ssq_k(c)
                if c < B - 2:
                    ctx_low(c + 2)
                if c == 2:
                    dve.wait_ge(small_in, 32)
                    dve.tensor_tensor(wqk[:, :], qn_sb[:, :], kn_sb[:, :], ALU.mult).then_inc(wqk_done, 1)
                    dve.wait_ge(wqk_done, 1)
                    dve.tensor_scalar(wqk[:, :], wqk[:, :], float(np.sqrt(HD)), None, ALU.mult).then_inc(wqk_done, 1)
                if c == 3:
                    nf_prep(0, 0, cols_of(0))
                if 0 <= c - 18 < B:
                    turn_x_lo(c - 18, c - 18)
                if 0 <= c - 1 < KV_SLABS * B:
                    norm_k(c - 1)
                if 0 <= c - 16 < B:
                    layer_norm(c - 16, c - 16)
                if c == 4:
                    dve.wait_ge(x_in, 16)
                if 0 <= c - 4 < B:
                    layer_stats(c - 4, c - 4)
                for q, t in early_bounds(c, 0):
                    chain(q, cols_of(q), t)
                    if t == 6 and q < Q0:
                        nf_prep(q + 1, (q + 1) % 3, cols_of(q + 1))
                if c >= KV_UNITS - 2:
                    sum_squares(0, c - KV_UNITS + 3)

            def step(g, s):
                mine = not isinstance(g, int) or g < G

                def chains(part):
                    for c, t in bounds_in(g, s, part, 0):
                        chain(Q0 + 3 * g + c, QC, t)

                if not in_phase0(g, s, 1):
                    sum_squares(g, s)
                chains(0)

                _, _, n = at(g, s, 2)
                if live(n):
                    r = n_par(s, 2)
                    dve.wait_ge(p_exp, n + 1)
                    dve.reciprocal(rsum[:, r, :], psum_[:, r, :]).then_inc(p_rsum, 1)

                chains(1)
                _, b, n = at(g, s, 4)
                if live(n):
                    dve.wait_ge(attn_ready, n + 1)
                    wait(dve, attn_added, n)
                    dve.tensor_tensor(resid[:, b, :], resid[:, b, :], attn_ps[:, :], ALU.add).then_inc(attn_added, 1)
                if mine and s in WO_STEP:
                    for j in WO_STEP[s]:
                        dve.wait_ge(wo_in[j], 16 * (g + 1))
                        wait(dve, attn_ready, B * (g - 1) if s < 2 else B * g)
                        if isinstance(g, int) and g == 0:
                            dve.wait_ge(kv_ready, KV_UNITS)
                        dve.tensor_copy(wo_part(0, g, j), wo_raw[:, j, :]).then_inc(wo_hi_done, 1)
                if mine and s < KT and not (isinstance(g, int) and g == G - 1):
                    first = isinstance(g, int) and g == 0
                    dve.wait_ge(raw_in[s], 16 * (2 * KV_SLABS + 2 + g))
                    dve.wait_ge(kv_ready if first else q_ready, KV_UNITS if first else B * g)
                    dve.tensor_copy(ring[:, (g + 1) % 2, 0, s, :], raw[:, s, :]).then_inc(slab_hi, 1)

                _, _, n = at(g, s, 3)
                if live(n):
                    r = n_par(s, 3)
                    dve.wait_ge(oT_hi, n + 1)
                    dve.tensor_tensor(o_lo_sb[:, r, :], oT_ps[:, :], o_hi_sb[:, r, :], ALU.subtract).then_inc(oT_lo, 1)

                _, _, n = at(g, s, 1)
                if live(n):
                    r = n_par(s, 1)
                    dve.wait_ge(s_ready, n + 1)
                    dve.wait_ge(q_rq, n + 1)
                    wait(dve, p_exp, n - 1)
                    if isinstance(n, int) and n == 0:
                        dve.wait_ge(mask_in, 16)
                    for j in range(J):
                        ins = dve.scalar_tensor_tensor(s_sb[:, r, j * S:(j + 1) * S], s_ps[r][:, j * S:(j + 1) * S],
                                                       rq[:, (s - 1) % 4, j:j + 1], mask_sb[:, :],
                                                       op0=ALU.mult, op1=ALU.add)
                    ins.then_inc(s_scaled, 1)
                    dve.wait_ge(s_scaled, n + 1)
                    dve.tensor_reduce(nmax[:, r, :], heads(s_sb[:, r, :]), AX.X, ALU.max, negate=True).then_inc(s_max, 1)

                chains(2)
                if mine and s in (0, 3):
                    nf_prep(Q0 + 3 * g + 1 + s // 3, 1 + s // 3, QC)
                if mine and s == 5 and not (isinstance(g, int) and g == G - 1):
                    nf_prep(Q0 + 3 * g + 3, 0, QC)

            for s in range(B):
                step(0, s)
            with dve.Fori(1, G - 1) as g:
                for s in range(B):
                    step(g, s)
            def stats_of(b):
                dve.wait_ge(attn_added, N - B + b + 1)
                layer_stats(B + b, b)

            for s in range(B):
                step(G - 1, s)
                if s >= 4:
                    stats_of(s - 4)
            def split_w(t, par, M, parts):
                for c in parts:
                    u = 3 * t + c
                    dve.wait_ge(w_hi, u + 1)
                    bank = wT_ps[(3 * par + c) % 2]
                    if c < 2:
                        dve.tensor_tensor(wT_part(par, c, 1, M), bank[:, 0:KT * M].rearrange("p (k m) -> p k m", k=KT),
                                          wT_part(par, c, 0, M), ALU.subtract).then_inc(w_lo, 1)
                    else:
                        dve.tensor_tensor(by_row(w3_part(par, 1, M)), heads(bank[0:M, :]), by_row(w3_part(par, 0, M)),
                                          ALU.subtract).then_inc(w_lo, 1)

            def hidden(t, M, half):
                v = 2 * t + half
                dve.wait_ge(silu_done, v + 1)
                dve.wait_ge(up_ready, v + 1)
                wait(dve, h_lo, v - 1)
                dve.tensor_tensor(h_sb[0:M, half, :], s_ps[half][0:M, :], silu_sb[0:M, half, :], ALU.mult).then_inc(h_done, 1)

            def add_down(t, m):
                last = isinstance(t, int) and t == TILES - 1
                n = LAST_ADD + m if last else len(ADDED) * t + ADDED.index(m)
                dve.wait_ge(down_ready, B * t + m + 1)
                if m in ADDED:
                    wait(dve, down_added, len(ADDED) * (t - 1) + ADDED.index(m) + 1)
                else:
                    dve.wait_ge(side_added, 2 * t - 1 + SIDE.index(m))
                dve.tensor_tensor(resid[:, m, :], resid[:, m, :], down_bank(t, m)[:, :], ALU.add).then_inc(down_added, 1)

            def ffn(t, par, quantise):
                def chains(lo, hi):
                    if quantise:
                        for n in range(lo, hi):
                            chain(t + (QF - FQ_STEP), QC, n)

                def adds(*batches):
                    if has_tile(t - 2):
                        last = isinstance(t, int) and t - 2 == TILES - 1
                        for m in batches:
                            if m in ADDED or last:
                                add_down(t - 2, m)

                if quantise:
                    nf_prep(t + (QF - FQ_STEP), 1 + par, QC, 2)
                if has_tile(t - 1):
                    split_w(t - 1, 1 - par, rows_of(t - 1), [2])
                chains(0, 2)
                adds(0, 1)
                chains(2, 4)
                if has_tile(t):
                    split_w(t, par, rows_of(t), [0])
                if isinstance(t, int) and t == 1:
                    for b in range(4, B):
                        turn_x_lo(B + b, b)
                chains(4, 5)
                if has_tile(t - 1):
                    hidden(t - 1, rows_of(t - 1), 0)
                adds(2, 3)
                chains(5, 10)
                adds(4, 5)
                if has_tile(t):
                    split_w(t, par, rows_of(t), [1])
                chains(10, 15)
                if has_tile(t - 1):
                    hidden(t - 1, rows_of(t - 1), 1)
                adds(6, 7)

            for s in range(4):
                if s == 3:
                    split_w(0, 0, P, [0, 1])
                step(G, s)
                stats_of(4 + s)
                if s == 0:
                    for b in range(4):
                        layer_norm(B + b, b)
                if s == 1:
                    for b in range(4):
                        turn_x_lo(B + b, b)
            for b in range(4, B):
                layer_norm(B + b, b)
            for t in range(1, FQ_STEP):
                ffn(t, t % 2, False)
            with dve.Fori(FQ_STEP // 2, (FQ_STEP + FQ) // 2) as tt:
                for par in range(2):
                    ffn(tt * 2 + par, par, True)
            for t in range(FQ_STEP + FQ, TILES + 2):
                ffn(t, t % 2, False)

        @block.gpsimd
        def _(pool):
            def low_part(dst, src, hi):
                return pool.tensor_tensor(dst, src, hi, ALU.subtract)

            def slab_part(m, k, dst):
                pool.wait_ge(slab_hi, KT * m + k + 1)
                low_part(dst[:, 1, k, :], raw[:, k, :], dst[:, 0, k, :]).then_inc(slab_lo, 1)

            def blocks(ap, cols):
                return ap.rearrange("p (b e) -> p b e", e=BLK)

            def nf_norm(q, slot, cols, slots=3):
                nb = cols // BLK
                pool.wait_ge(nf_rmax, q + 1)
                wait(pool, nf_signed, BOUNDS * (q - slots + 1))
                pool.tensor_tensor(blocks(nf_n[:, slot, 0:cols], cols), blocks(nf_raw[:, 0:cols], cols),
                                   rmax[:, 0:nb].unsqueeze(2).to_broadcast([P, nb, BLK]), ALU.mult).then_inc(nf_normed, 1)

            def nf_sum(q, cols):
                pool.wait_ge(nf_chained, BOUNDS * (q + 1))
                wait(pool, nf_out, 16 * q)
                pool.tensor_tensor(nf_dq[:, 0:cols], nf_pos[:, 0:cols], nf_neg[:, 0:cols], ALU.add).then_inc(nf_summed, 1)

            def nf_scale(q, slot, cols):
                nb = cols // BLK
                pool.wait_ge(nf_summed, q + 1)
                v = blocks(nf_dq[:, 0:cols], cols)
                pool.tensor_tensor(v, v, safe[:, slot, 0:nb].unsqueeze(2).to_broadcast([P, nb, BLK]), ALU.mult)\
                    .then_inc(nf_scaled, 1)

            pool.memset(ident[:, :], 0.0).then_inc(const_zero, 1)
            pool.memset(neg_half[:, :], -0.5).then_inc(const_set, 1)
            pool.memset(hd_eps[:, :], HD * EPS).then_inc(const_set, 1)
            pool.memset(ln_eps[:, :], LN_EPS).then_inc(const_set, 1)
            pool.wait_ge(const_zero, 1)
            pool.affine_select(out=ident[:, :], in_=ident[:, :], compare_op=ALU.not_equal, fill=1.0, base=0,
                               pattern=[[-1, P]], channel_multiplier=1).then_inc(const_done, 1)
            pool.wait_ge(const_set, 3)

            def rms(n, slot, ssq_sem, var_sem, out_sem):
                pool.wait_ge(ssq_sem, n + 1)
                wait(pool, out_sem, n)
                pool.tensor_tensor(var[:, :], ssq[:, slot, :], hd_eps[:, :], ALU.add).then_inc(var_sem, 1)
                pool.wait_ge(var_sem, n + 1)
                pool.tensor_tensor(rq[:, slot, :], var[:, :], neg_half[:, 0:J], ALU.pow).then_inc(out_sem, 1)

            def ln_scale(r):
                half = slice(4 * (r % 2), 4 * (r % 2) + 4)
                pool.wait_ge(ln_mv, 4 * (r + 1))
                pool.tensor_tensor(ln_var_sb[:, half], mv[:, half, 1], ln_eps[:, :], ALU.add).then_inc(ln_var, 1)
                pool.wait_ge(ln_var, r + 1)
                pool.tensor_tensor(rstd[:, half], ln_var_sb[:, half], neg_half[:, 0:4], ALU.pow).then_inc(ln_rstd, 1)

            def rms_queries(g, s):
                _, _, n = at(g, s, 1)
                if live(n):
                    wait(pool, s_scaled, n - 3)
                    rms(n, (s - 1) % 4, q_ssq, q_var, q_rq)

            for c in range(KV_UNITS):
                m, b, is_k = kv_kind(c)
                if is_k:
                    wait(pool, k_normed, c - 3)
                    rms(c, c % 4, kv_ssq, kv_var, kv_rk)
                if c == 3:
                    nf_norm(0, 0, cols_of(0))
                if c in (8, 12):
                    ln_scale(c // 4 - 2)
                if 0 <= c - 2 < KT:
                    if c == 2:
                        pool.wait_ge(slab_lo, KT)
                    slab_part(1, c - 2, slab_slot(1))
                if 1 <= m < 4 and b < KT:
                    slab_part(m + 1, b, slab_slot(m + 1))
                for q, t in early_bounds(c, 0):
                    if t == 8 and q < Q0:
                        nf_norm(q + 1, (q + 1) % 3, cols_of(q + 1))
                    if t == BOUNDS - 1:
                        nf_sum(q, cols_of(q))
                        nf_scale(q, q % 3, cols_of(q))
                if c >= KV_UNITS - 2:
                    rms_queries(0, c - KV_UNITS + 3)

            def step(g, s):
                q = Q0 + 3 * g
                mine = not isinstance(g, int) or g < G
                last = isinstance(g, int) and g == G - 1
                if not in_phase0(g, s, 1):
                    rms_queries(g, s)
                _, _, n = at(g, s, 2)
                if live(n):
                    r = n_par(s, 2)
                    pool.wait_ge(p_rsum, n + 1)
                    v = heads(p_sb[:, r, :])
                    pool.tensor_tensor(v, v, rsum[:, r, :].unsqueeze(2).to_broadcast([P, J, S]), ALU.mult)\
                        .then_inc(p_normed, 1)
                if mine and s in WO_STEP:
                    for j in WO_STEP[s]:
                        pool.wait_ge(wo_hi_done, J * g + j + 1)
                        low_part(wo_part(1, g, j), wo_raw[:, j, :], wo_part(0, g, j)).then_inc(wo_lo_done, 1)
                if mine and s in (1, 4):
                    nf_norm(q + (s + 2) // 3, (s + 2) // 3, QC)
                if mine and s == 6 and not last:
                    nf_norm(q + 3, 0, QC)
                if mine and s in (3, 6):
                    nf_scale(q + s // 3 - 1, s // 3 - 1, QC)
                if s == 0 and not (isinstance(g, int) and g in (0, G)):
                    nf_scale(q - 1, 2, QC)
                if mine and s < KT and not last:
                    slab_part(2 * KV_SLABS + 1 + g, s, ring[:, (g + 1) % 2, :, :, :])
                if mine and s in (2, 5, 7):
                    nf_sum(q + s // 3, QC)

            for s in range(B):
                step(0, s)
            with pool.Fori(1, G - 1) as g:
                for s in range(B):
                    step(g, s)
            for s in range(B):
                step(G - 1, s)
            for s in range(4):
                step(G, s)
                if s == 0:
                    ln_scale(2)
            ln_scale(3)

            def hidden_lo(t, par, M, half):
                pool.wait_ge(h_hi, 2 * t + half + 1)
                low_part(hT_lo[0:M, par, half * 512:(half + 1) * 512], h_sb[0:M, half, :],
                         hT_hi[0:M, par, half * 512:(half + 1) * 512]).then_inc(h_lo, 1)

            def add_side(t, half):
                n = 2 * t + half
                m = SIDE[half]
                pool.wait_ge(side_copied, n + 1)
                wait(pool, side_added, n)
                pool.tensor_tensor(resid[:, m, :], resid[:, m, :], side_sb[:, half, :], ALU.add).then_inc(side_added, 1)

            def ffn(t, par, quantise, scale_last):
                q = t + (QF - FQ_STEP)
                if quantise:
                    nf_norm(q, 1 + par, QC, 2)
                if scale_last:
                    nf_scale(q - 1, 2 - par, QC)
                if has_tile(t - 2):
                    hidden_lo(t - 2, par, rows_of(t - 2), 1)
                if has_side(t - 3):
                    add_side(t - 3, 1)
                if has_tile(t - 1):
                    hidden_lo(t - 1, 1 - par, rows_of(t - 1), 0)
                if has_side(t - 2):
                    add_side(t - 2, 0)
                if quantise:
                    nf_sum(q, QC)

            for t in range(FQ_STEP):
                ffn(t, t % 2, False, False)
            with pool.Fori(FQ_STEP // 2, (FQ_STEP + FQ) // 2) as tt:
                for par in range(2):
                    ffn(tt * 2 + par, par, True, True)
            for t in range(FQ_STEP + FQ, TILES + 3):
                ffn(t, t % 2, False, t == FQ_STEP + FQ)


_OUT = ((B, S, D), "float32")


def kernel(**inputs):
    import numpy as _np
    import concourse.bacc as _bacc
    from concourse import mybir as _mybir
    from concourse.bass_utils import run_bass_kernel_spmd as _run

    a = {k: _np.asarray(v) for k, v in inputs.items()}
    w12 = _np.zeros((2, TILES * P, D), a["L0_ffn_w1"].dtype)
    w12[0, :F], w12[1, :F] = a["L0_ffn_w1"], a["L0_ffn_w2"]
    w12 = w12.reshape(2, TILES, P, D).transpose(2, 1, 0, 3).reshape(P, TILES * 2 * D)
    laid = {
        "x": a["x"],
        "ctxT": a["ctx_4096"].reshape(B * S, D).T,
        "mask": a["mask_1x1xSxS2_ff0"],
        "wqT": a["L0_xattn_q_proj_w"].T,
        "wkT": a["L0_xattn_k_proj_w"].T,
        "wvT": a["L0_xattn_v_proj_w"].T,
        "woT": a["L0_xattn_o_proj_w"].T,
        "qnw": a["L0_xattn_q_norm_w"],
        "knw": a["L0_xattn_k_norm_w"],
        "wff": _np.concatenate([a["L0_ffn_w3"].reshape(P, FLAT), w12], axis=1),
    }
    nc = _bacc.Bacc("TRN2", target_bir_lowering=False, num_devices=1)
    arrays, args = {}, []
    for name, v in laid.items():
        v = _np.ascontiguousarray(v)
        arrays[f"in_{name}"] = v
        args.append(nc.dram_tensor(f"in_{name}", v.shape, _mybir.dt.from_np(v.dtype), kind="ExternalInput").ap())
    out = nc.dram_tensor("out_0", _OUT[0], _mybir.dt.from_np(_np.dtype(_OUT[1])), kind="ExternalOutput").ap()
    build(nc, *args, out)
    r = _run(nc, [arrays], core_ids=[0])
    return r.results[0]["out_0"]
```
